# Optimizing a Trainium2 kernel written in Bass

```python
import numpy as np
import jax
import jax.numpy as jnp

def _softmax(x, axis=-1):
    return jax.nn.softmax(x, axis=axis)
def _gelu(x):
    return jax.nn.gelu(x, approximate=True)
def _silu(x):
    return jax.nn.silu(x)
def _sigmoid(x):
    return jax.nn.sigmoid(x)
def _layernorm(x, axis=-1, eps=1e-5):
    m = jnp.mean(x, axis=axis, keepdims=True)
    v = jnp.var(x, axis=axis, keepdims=True)
    return (x - m) / jnp.sqrt(v + eps)
def _scatter_add(tgt, idx, src, axis=0):
    return tgt.at[idx].add(src)
def _segment_sum(src, seg, n):
    return jax.ops.segment_sum(src, seg, n)

kernel_name = 'mk_adj_preln_d1_adj_512_981dc4'

def setup_inputs(seed: int = 0):
    np.random.seed(seed)
    _w = jnp.asarray
    def _rec_inputs():
        import jax
        import jax.numpy as jnp
        _gk = jax.random.key(seed)
        x = 7.22e-05 + 1 * jax.random.normal(jax.random.fold_in(_gk, 1), (16, 1024, 512), jnp.float32)
        _a = jax.random.bernoulli(jax.random.fold_in(_gk, 2), 0.00390625, (16, 1024, 1024))
        _a = jnp.logical_or(_a, jnp.swapaxes(_a, -1, -2))
        _a = jnp.logical_or(_a, jnp.eye(1024, dtype=bool))
        _af = _a.astype(jnp.float32)
        _af = _af * jax.random.uniform(jax.random.fold_in(_gk, 3), (16, 1024, 1024), jnp.float32, 0.05, 1)
        adj = _af
        return x, adj
    x, adj = _rec_inputs()
    def _L0_gnn_setup():
        import jax, jax.numpy as jnp
        import numpy as np
        B, N, D = (8, 2048, 512)
        key = jax.random.key(seed)
        ks = jax.random.split(key, 8)
        scale = 0.5 / np.sqrt(D)
        x = jax.random.normal(ks[0], (B, N, D), dtype=jnp.float32)
        adj = jax.random.uniform(ks[1], (B, N, N), dtype=jnp.float32)
        Wq_w = jax.random.normal(ks[2], (D, D), dtype=jnp.float32) * scale
        Wk_w = jax.random.normal(ks[3], (D, D), dtype=jnp.float32) * scale
        Wv_w = jax.random.normal(ks[4], (D, D), dtype=jnp.float32) * scale
        Wq_b = jnp.zeros((D,), dtype=jnp.float32)
        Wk_b = jnp.zeros((D,), dtype=jnp.float32)
        Wv_b = jnp.zeros((D,), dtype=jnp.float32)
        return {'x': x, 'adj': adj, 'Wq_w': Wq_w, 'Wq_b': Wq_b, 'Wk_w': Wk_w, 'Wk_b': Wk_b, 'Wv_w': Wv_w, 'Wv_b': Wv_b}
    _L0_gnn_all = _L0_gnn_setup()
    _L0_gnn_in = {k: v for k, v in _L0_gnn_all.items() if k in ('Wq_w', 'Wq_b', 'Wk_w', 'Wk_b', 'Wv_w', 'Wv_b', )}
    del _L0_gnn_all

    return {
        "x": x,
        "adj": adj,
        "L0_gnn_Wq_w": _L0_gnn_in["Wq_w"],
        "L0_gnn_Wq_b": _L0_gnn_in["Wq_b"],
        "L0_gnn_Wk_w": _L0_gnn_in["Wk_w"],
        "L0_gnn_Wk_b": _L0_gnn_in["Wk_b"],
        "L0_gnn_Wv_w": _L0_gnn_in["Wv_w"],
        "L0_gnn_Wv_b": _L0_gnn_in["Wv_b"],
    }

def reference(x, adj, L0_gnn_Wq_w, L0_gnn_Wq_b, L0_gnn_Wk_w, L0_gnn_Wk_b, L0_gnn_Wv_w, L0_gnn_Wv_b):
    import jax
    import jax.numpy as jnp
    def _L0_gnn_ref(x, adj, Wq_w, Wq_b, Wk_w, Wk_b, Wv_w, Wv_b):
        import jax, jax.numpy as jnp
        import numpy as np
        B, N, D = (8, 2048, 512)
        query = jnp.einsum('bnd,od->bno', x, Wq_w) + Wq_b
        keyt = jnp.einsum('bnd,od->bno', x, Wk_w) + Wk_b
        value = jnp.einsum('bnd,od->bno', x, Wv_w) + Wv_b
        weight = jnp.einsum('bqd,bkd->bqk', query, keyt)
        weight = adj * jnp.exp(weight)
        weight = weight / jnp.sum(weight, axis=2, keepdims=True)
        return jnp.einsum('bqk,bkd->bqd', weight, value)

    h = jnp.maximum(_layernorm(x, axis=-1), 0.0)
    x = x + _L0_gnn_ref(h, adj, L0_gnn_Wq_w, L0_gnn_Wq_b, L0_gnn_Wk_w, L0_gnn_Wk_b, L0_gnn_Wv_w, L0_gnn_Wv_b)
    return x


_drawn_inputs = setup_inputs


def setup_inputs(seed=0):
    import zlib

    import numpy as np

    out = dict(_drawn_inputs(seed))
    spreads = {'L0_gnn_Wq_b': (0.0, 0.1), 'L0_gnn_Wk_b': (0.0, 0.1), 'L0_gnn_Wv_b': (0.0, 0.1)}
    factors = {}
    for name, (base, spread) in spreads.items():
        noise = np.random.default_rng([zlib.crc32(name.encode()), seed]).standard_normal(out[name].shape)
        drawn = base * np.exp(spread * noise) if base else spread * noise
        out[name] = jnp.asarray(drawn.astype(out[name].dtype))
    for name, factor in factors.items():
        out[name] = (out[name] * factor).astype(out[name].dtype)
    return out
```

```python
from contextlib import ExitStack

import concourse.bass as bass
from concourse import mybir



def adjacency_attention_kernel(nc, x, adj, wq, bq, wk, bk, wv, bv, out):
    ALU = mybir.AluOpType
    ACT = mybir.ActivationFunctionType
    F32 = mybir.dt.float32
    F32R = mybir.dt.float32r
    P = 128
    EPS = 1e-5
    B, N, D = x.shape
    BANK = 512
    TILES = N // P
    CH = D // P
    HALVES = N // BANK
    TPH = TILES // HALVES
    GROUPS = CH * HALVES
    UNITS = HALVES * TILES
    SQ = 32
    QUADS = P // SQ
    RING = 4
    LAG = 3
    assert D == BANK and HALVES == 2 and TPH == CH == QUADS == 4 and B % 2 == 0

    H_BANK = [(0, 1, 3)[g % 3] for g in range(GROUPS)]
    U_BANK = [(3, 0, 1, 2)[g % 4] for g in range(GROUPS)]
    V_BANK = U_BANK
    SUM_BANK = 2

    x_rows = x.rearrange("b (M p m) d -> b p M (m d)", p=P, m=TPH)
    out_rows = out.rearrange("b (M p m) d -> b p M (m d)", p=P, m=TPH)
    adj_blocks = adj.rearrange("b (Q a c m) (K g j) -> b K g Q c m a j", Q=HALVES, a=QUADS, m=TPH, K=HALVES, g=QUADS)

    with ExitStack() as ctx:
        def sb(name, shape, dt=F32):
            return ctx.enter_context(nc.sbuf_tensor(name, shape, dt))

        def sem(name):
            return ctx.enter_context(nc.semaphore(name))

        mT_hi = sb("mT_hi", [P, CH, D], F32R)
        mT_lo = sb("mT_lo", [P, CH, D], F32R)
        wvT_hi = sb("wvT_hi", [P, CH, D], F32R)
        wvT_lo = sb("wvT_lo", [P, CH, D], F32R)
        hT_hi = sb("hT_hi", [P, CH, N], F32R)
        hT_lo = sb("hT_lo", [P, CH, N], F32R)
        uT_hi = sb("uT_hi", [P, CH, N], F32R)
        uT_lo = sb("uT_lo", [P, CH, N], F32R)
        v_hi = sb("v_hi", [P, TILES, D], F32R)
        v_lo = sb("v_lo", [P, TILES, D], F32R)
        pT_hi = sb("pT_hi", [P, RING, BANK], F32R)
        pT_lo = sb("pT_lo", [P, RING, BANK], F32R)
        xn = sb("xn", [P, TILES, D])
        res = sb("res", [P, TPH, D])
        adj_in = sb("adj_in", [P, HALVES, TILES * QUADS // 2, P])
        prob = sb("prob", [P, RING, BANK])
        e_sb = sb("e_sb", [P, 2, BANK])
        prob_sum = sb("prob_sum", [P, BANK])
        ident = sb("ident", [P, P])
        ones = sb("ones", [P, 1])
        c_rep = sb("c_rep", [P, D])
        bv_rep = sb("bv_rep", [P, D])
        products = sb("products", [P, D])
        a_col = sb("a_col", [P, CH])
        bqk = sb("bqk", [P, 1])
        bq_col = sb("bq_col", [P, CH])
        bk_col = sb("bk_col", [P, CH])
        stats = sb("stats", [P, TILES, 6])
        mean_var = sb("mean_var", [P, TILES, 2])
        var_eps = sb("var_eps", [P, TILES])
        minus_half = sb("minus_half", [P, TILES])
        rstd = sb("rstd", [P, TILES])
        s_raw = sb("s_raw", [P, TILES])
        s_col = sb("s_col", [P, TILES])
        row_inv = sb("row_inv", [P, TILES])
        wk_in = adj_in[:, 0].rearrange("p (c e) q -> p c (e q)", c=CH)
        wq_in = adj_in[:, 1].rearrange("p (c e) q -> p c (e q)", c=CH)
        wv_in = res
        bq_rep = e_sb[:, 0].rearrange("p (c q) -> p c q", c=CH)

        work = ctx.enter_context(nc.psum_tensor("work", [P, 4, BANK], F32))
        o_ps = ctx.enter_context(nc.psum_tensor("o_ps", [P, TPH, BANK], F32))

        wqk_loaded = [sem(f"wqk{c}_loaded") for c in range(CH)]
        biases_loaded = sem("biases_loaded")
        wv_loaded = sem("wv_loaded")
        bv_loaded = sem("bv_loaded")
        x_loaded = [sem("x_half0_loaded"), sem("x_half1_loaded")]
        adj_loaded = [sem("adj_half0_loaded"), sem("adj_half1_loaded")]
        res_loaded = sem("res_loaded")
        out_stored = sem("out_stored")
        consts_ready = sem("consts_ready")
        rstd_ready = sem("rstd_ready")
        sum_ready = sem("sum_ready")
        res_bv_ready = sem("res_bv_ready")
        mT_done = sem("mT_done")
        wb_done = sem("wb_done")
        wvT_done = sem("wvT_done")
        hT_done = sem("hT_done")
        uT_done = sem("uT_done")
        v_done = sem("v_done")
        scores_done = sem("scores_done")
        row_sums_done = sem("row_sums_done")
        o_done = sem("o_done")
        w_hi_ready = sem("w_hi_ready")
        hT_hi_ready = sem("hT_hi_ready")
        uT_hi_ready = sem("uT_hi_ready")
        v_hi_ready = sem("v_hi_ready")
        exp_ready = sem("exp_ready")
        pT_hi_ready = sem("pT_hi_ready")
        bq_rep_ready = sem("bq_rep_ready")
        w_lo_ready = sem("w_lo_ready")
        wb_ready = sem("wb_ready")
        stats_done = sem("stats_done")
        mean_var_done = sem("mean_var_done")
        var_ready = sem("var_ready")
        xn_ready = sem("xn_ready")
        s_raw_done = sem("s_raw_done")
        s_ready = sem("s_ready")
        hT_lo_ready = sem("hT_lo_ready")
        uT_lo_ready = sem("uT_lo_ready")
        v_lo_ready = sem("v_lo_ready")
        adjT_ready = sem("adjT_ready")
        prob_ready = sem("prob_ready")
        pT_lo_ready = sem("pT_lo_ready")
        row_inv_ready = sem("row_inv_ready")
        out_ready = sem("out_ready")

        def summed(b, u):
            half, i = divmod(u, TILES)
            return (TILES - 1) * (HALVES * b + half) + max(i, 1)

        block = ctx.enter_context(nc.Block())

        @block.sync
        def _(sp):
            def load_x(b):
                for half in range(HALVES):
                    sp.dma_start(xn[:, half * TPH:(half + 1) * TPH], x_rows[b, :, half]
                                 .rearrange("p (m d) -> p m d", d=D)).then_inc(x_loaded[half], 16)

            def load_adj(b, n):
                queries, keys = divmod(n, HALVES)
                for g in range(QUADS):
                    sp.dma_start(adj_in[g * SQ:(g + 1) * SQ, keys].rearrange("c (m a) j -> c m a j", m=TPH),
                                 adj_blocks[b, keys, g, queries]).then_inc(adj_loaded[keys], 16)

            def load_res(b, half):
                sp.dma_start(res[:, :, :], x_rows[b, :, half].rearrange("p (m d) -> p m d", d=D)
                             ).then_inc(res_loaded, 16)

            def store_out(b, half):
                sp.wait_ge(out_ready, TILES * b + TPH * (half + 1))
                sp.dma_start(out_rows[b, :, half].rearrange("p (m d) -> p m d", d=D), res[:, :, :]
                             ).then_inc(out_stored, 16)
                sp.wait_ge(out_stored, 16 * HALVES * b + 16 * (half + 1))

            def graph(b, following):
                if following:
                    sp.wait_ge(hT_done, GROUPS * b + GROUPS)
                    sp.wait_ge(s_raw_done, TILES * b + TILES)
                    load_x(b + 1)
                for n in range(2 * HALVES):
                    if n == HALVES + 1:
                        store_out(b, 0)
                        load_res(b, 1)
                    if n < HALVES or following:
                        sp.wait_ge(adjT_ready, UNITS * b + TPH * (n + 1))
                        if n < HALVES:
                            load_adj(b, n + HALVES)
                        else:
                            load_adj(b + 1, n - HALVES)
                store_out(b, 1)
                if following:
                    load_res(b + 1, 0)

            for c in range(CH):
                rows = slice(c * P, (c + 1) * P)
                sp.dma_start(wk_in[:, c], wk[rows, :]).then_inc(wqk_loaded[c], 16)
                sp.dma_start(wq_in[:, c], wq[rows, :]).then_inc(wqk_loaded[c], 16)
            sp.wait_ge(wb_done, 1)
            load_adj(0, 0)
            load_adj(0, 1)
            sp.wait_ge(wvT_done, CH)
            load_res(0, 0)
            with sp.Fori(0, B - 1) as b:
                graph(b, True)
            graph(B - 1, False)

        @block.gpsimd
        def _(pool):
            def reciprocal_std(b):
                pool.wait_ge(var_ready, b + 1)
                pool.tensor_tensor(rstd[:, :], var_eps[:, :], minus_half[:, :], ALU.pow).then_inc(rstd_ready, 1)

            def graph(b, following):
                for half in range(HALVES):
                    for i in range(TILES):
                        u = half * TILES + i
                        if i >= 2:
                            pool.wait_ge(sum_ready, summed(b, u - 1))
                        if u == TILES + 1:
                            pool.wait_ge(row_sums_done, HALVES * b + 1)
                        if i >= 1:
                            before = prob[:, (u - 1) % RING] if i == 1 else prob_sum[:, :]
                            pool.wait_ge(prob_ready, UNITS * b + u + 1)
                            pool.tensor_tensor(prob_sum[:, :], before, prob[:, u % RING], ALU.add
                                               ).then_inc(sum_ready, 1)
                        if 2 <= i < 2 + TPH:
                            m = i - 2
                            if m == 0:
                                pool.wait_ge(res_loaded, 16 * HALVES * b + 16 * (half + 1))
                            pool.tensor_tensor(res[:, m], res[:, m], bv_rep[:, :], ALU.add
                                               ).then_inc(res_bv_ready, 1)
                        if following and u == TPH + 3:
                            reciprocal_std(b + 1)

            pool.memset(ident[:, :], 0.0).then_inc(consts_ready, 1)
            pool.memset(minus_half[:, :], -0.5).then_inc(consts_ready, 1)
            pool.memset(ones[:, :], 1.0).then_inc(consts_ready, 1)
            pool.wait_ge(consts_ready, 3)
            pool.affine_select(out=ident[:, :], in_=ident[:, :], compare_op=ALU.not_equal, fill=1.0,
                               base=0, pattern=[[-1, P]], channel_multiplier=1).then_inc(consts_ready, 1)
            reciprocal_std(0)
            pool.wait_ge(bv_loaded, 16)
            with pool.Fori(0, B - 1) as b:
                graph(b, True)
            graph(B - 1, False)

        @block.scalar
        def _(act):
            def hidden_hi(b, g):
                act.wait_ge(hT_done, GROUPS * b + g + 1)
                half, c = divmod(g, CH)
                act.activation(hT_hi[:, c, half * BANK:(half + 1) * BANK], work[:, H_BANK[g]], ACT.Relu
                               ).then_inc(hT_hi_ready, 1)

            def graph(b, following):
                for g in range(GROUPS):
                    act.wait_ge(uT_done, GROUPS * b + g + 1)
                    half, c = divmod(g, CH)
                    act.activation(uT_hi[:, c, half * BANK:(half + 1) * BANK], work[:, U_BANK[g]], ACT.Identity,
                                   bias=a_col[:, c:c + 1]).then_inc(uT_hi_ready, 1)
                for i in range(TILES):
                    act.wait_ge(v_done, TILES * b + i + 1)
                    act.activation(v_hi[:, i], work[:, V_BANK[i]], ACT.Copy).then_inc(v_hi_ready, 1)
                act.wait_ge(s_ready, b + 1)
                for u in range(UNITS):
                    i = u % TILES
                    if u >= 2:
                        act.wait_ge(prob_ready, UNITS * b + u - 1)
                    act.wait_ge(scores_done, UNITS * b + u + 1)
                    act.activation(e_sb[:, u % 2], work[:, u % 2], ACT.Exp, bias=s_col[:, i:i + 1]
                                   ).then_inc(exp_ready, 1)
                    act.wait_ge(prob_ready, UNITS * b + u + 1)
                    act.activation(pT_hi[:, u % RING], prob[:, u % RING], ACT.Copy).then_inc(pT_hi_ready, 1)
                if following:
                    for g in range(GROUPS):
                        hidden_hi(b + 1, g)

            act.dma_start(bk_col[:, :], bk.rearrange("(c p) -> p c", p=P), allow_slow_non_contiguous=True
                          ).then_inc(biases_loaded, 16)
            act.dma_start(bq_col[:, :], bq.rearrange("(c p) -> p c", p=P), allow_slow_non_contiguous=True
                          ).then_inc(biases_loaded, 16)
            for half in range(HALVES):
                act.dma_start(xn[:, half * TPH:(half + 1) * TPH],
                              x_rows[0, :, half].rearrange("p (m d) -> p m d", d=D)).then_inc(x_loaded[half], 16)
            act.dma_start(wv_in[:, :, :], wv.rearrange("(c p) d -> p c d", p=P)).then_inc(wv_loaded, 16)
            act.dma_start(bv_rep[:, :], bv.rearrange("(a d) -> a d", a=1).partition_broadcast(P)
                          ).then_inc(bv_loaded, 16)
            act.wait_ge(mT_done, 1)
            for c in range(CH):
                act.activation(mT_hi[:, c], work[:, c], ACT.Copy).then_inc(w_hi_ready, 1)
            for c in range(CH):
                act.wait_ge(wvT_done, c + 1)
                act.activation(wvT_hi[:, c], o_ps[:, c], ACT.Copy).then_inc(w_hi_ready, 1)
            for g in range(GROUPS):
                hidden_hi(0, g)
            act.wait_ge(wb_ready, 1)
            with act.Fori(0, B - 1) as b:
                graph(b, True)
            graph(B - 1, False)

        @block.vector
        def _(dve):
            def row_stats(tiles):
                for i in tiles:
                    dve.bn_stats(stats[:, i], xn[:, i]).then_inc(stats_done, 1)

            def mean_and_variance(tiles):
                for i in tiles:
                    dve.bn_aggr(mean_var[:, i], stats[:, i]).then_inc(mean_var_done, 1)

            def variance(b):
                dve.wait_ge(mean_var_done, TILES * b + TILES)
                dve.tensor_scalar(var_eps[:, :], mean_var[:, :, 1], EPS, None, ALU.add).then_inc(var_ready, 1)

            def normalise(tiles):
                for i in tiles:
                    dve.tensor_scalar(xn[:, i], xn[:, i], mean_var[:, i, 0:1], rstd[:, i:i + 1],
                                      ALU.subtract, ALU.mult).then_inc(xn_ready, 1)

            def key_terms(b, tiles):
                for i in tiles:
                    dve.wait_ge(xn_ready, TILES * b + i + 1)
                    if not (isinstance(b, int) and b == i == 0):
                        dve.wait_ge(s_raw_done, TILES * b + i)
                    dve.scalar_tensor_tensor(out=products[:, :], in0=xn[:, i], scalar=0.0, in1=c_rep[:, :],
                                             op0=ALU.max, op1=ALU.mult, accum_out=s_raw[:, i:i + 1]
                                             ).then_inc(s_raw_done, 1)

            def key_bias(b):
                dve.wait_ge(s_raw_done, TILES * b + TILES)
                dve.tensor_scalar(s_col[:, :], s_raw[:, :], bqk[:, 0:1], None, ALU.add).then_inc(s_ready, 1)

            def hidden_lo(b, g):
                dve.wait_ge(hT_hi_ready, GROUPS * b + g + 1)
                half, c = divmod(g, CH)
                cols = slice(half * BANK, (half + 1) * BANK)
                dve.scalar_tensor_tensor(out=hT_lo[:, c, cols], in0=work[:, H_BANK[g]], scalar=0.0,
                                         in1=hT_hi[:, c, cols].bitcast(F32), op0=ALU.max, op1=ALU.subtract
                                         ).then_inc(hT_lo_ready, 1)

            def transpose_adj(b, u):
                queries, i = divmod(u, TILES)
                keys, m = divmod(i, TPH)
                if m == 0:
                    dve.wait_ge(adj_loaded[keys], 16 * QUADS * (HALVES * b + queries + 1))
                if u >= RING:
                    dve.wait_ge(sum_ready, summed(b, u - RING))
                    dve.wait_ge(pT_lo_ready, UNITS * b + u - RING + 1)
                dve.transpose(prob[:, u % RING].rearrange("p (n c) -> p n c", c=SQ),
                              adj_in[:, keys].rearrange("p n (r m) -> p n r m", m=TPH)[:, :, :, m]
                              ).then_inc(adjT_ready, 1)

            def results(b, half):
                dve.wait_ge(row_sums_done, HALVES * b + half + 1)
                cols = slice(half * TPH, (half + 1) * TPH)
                dve.reciprocal(row_inv[:, cols], work[:, SUM_BANK, cols]).then_inc(row_inv_ready, 1)
                dve.wait_ge(row_inv_ready, HALVES * b + half + 1)
                for m in range(TPH):
                    n = half * TPH + m
                    dve.wait_ge(res_bv_ready, TILES * b + n + 1)
                    dve.wait_ge(o_done, TILES * b + n + 1)
                    dve.scalar_tensor_tensor(out=res[:, m], in0=o_ps[:, m], scalar=row_inv[:, n:n + 1],
                                             in1=res[:, m], op0=ALU.mult, op1=ALU.add).then_inc(out_ready, 1)

            def graph(b, following):
                for g in range(GROUPS):
                    dve.wait_ge(uT_hi_ready, GROUPS * b + g + 1)
                    half, c = divmod(g, CH)
                    cols = slice(half * BANK, (half + 1) * BANK)
                    dve.scalar_tensor_tensor(out=uT_lo[:, c, cols], in0=work[:, U_BANK[g]],
                                             scalar=a_col[:, c:c + 1], in1=uT_hi[:, c, cols].bitcast(F32),
                                             op0=ALU.add, op1=ALU.subtract).then_inc(uT_lo_ready, 1)
                for i in range(TILES):
                    dve.wait_ge(v_hi_ready, TILES * b + i + 1)
                    dve.tensor_tensor(v_lo[:, i], work[:, V_BANK[i]], v_hi[:, i].bitcast(F32),
                                      ALU.subtract).then_inc(v_lo_ready, 1)
                    if i < 2:
                        transpose_adj(b, i)
                for u in range(UNITS):
                    dve.wait_ge(exp_ready, UNITS * b + u + 1)
                    dve.wait_ge(adjT_ready, UNITS * b + u + 1)
                    dve.tensor_tensor(prob[:, u % RING], e_sb[:, u % 2], prob[:, u % RING], ALU.mult
                                      ).then_inc(prob_ready, 1)
                    if u + 2 < UNITS:
                        transpose_adj(b, u + 2)
                    aggregated = following and 2 <= u <= TILES // 2 + 1
                    if aggregated:
                        dve.wait_ge(stats_done, TILES * (b + 1) + 2 * u - 2)
                    if following and u == TILES:
                        dve.wait_ge(rstd_ready, b + 2)
                    dve.wait_ge(pT_hi_ready, UNITS * b + u + 1)
                    dve.tensor_tensor(pT_lo[:, u % RING], prob[:, u % RING], pT_hi[:, u % RING].bitcast(F32),
                                      ALU.subtract).then_inc(pT_lo_ready, 1)
                    if following:
                        if aggregated:
                            mean_and_variance([2 * u - 4, 2 * u - 3])
                        if u in (1, TPH // 2 + 1):
                            dve.wait_ge(x_loaded[u // 2], 16 * b + 32)
                        if 1 <= u <= TILES // 2:
                            row_stats([2 * u - 2, 2 * u - 1])
                        if u == TILES // 2 + 1:
                            variance(b + 1)
                        if u in (TILES, TILES + 1):
                            normalise(range((u - TILES) * TPH, (u - TILES + 1) * TPH))
                        if TILES + LAG <= u < TILES + LAG + 4:
                            key_terms(b + 1, [2 * (u - TILES - LAG), 2 * (u - TILES - LAG) + 1])
                    if u == TILES + LAG - 1:
                        results(b, 0)
                if following:
                    for g in range(GROUPS):
                        hidden_lo(b + 1, g)
                    key_bias(b + 1)
                results(b, 1)

            dve.wait_ge(biases_loaded, 32)
            for c in range(CH):
                last = dve.tensor_copy(bq_rep[:, c], bq_col[:, c:c + 1].broadcast_to([P, P]))
            last.then_inc(bq_rep_ready, 1)
            for half in range(HALVES):
                dve.wait_ge(x_loaded[half], 16)
                row_stats(range(half * TPH, (half + 1) * TPH))
            dve.wait_ge(stats_done, TILES)
            mean_and_variance(range(TILES))
            variance(0)
            for c in range(CH):
                dve.wait_ge(w_hi_ready, c + 1)
                dve.tensor_tensor(mT_lo[:, c], work[:, c], mT_hi[:, c].bitcast(F32), ALU.subtract
                                  ).then_inc(w_lo_ready, 1)
            dve.wait_ge(rstd_ready, 1)
            normalise(range(TILES))
            for c in range(CH):
                dve.wait_ge(w_hi_ready, CH + c + 1)
                dve.tensor_tensor(wvT_lo[:, c], o_ps[:, c], wvT_hi[:, c].bitcast(F32), ALU.subtract
                                  ).then_inc(w_lo_ready, 1)
            for g in range(GROUPS):
                hidden_lo(0, g)
            dve.wait_ge(wb_done, 1)
            dve.tensor_copy(c_rep[:, :], o_ps[:, 0])
            dve.tensor_copy(a_col[:, :], work[:, SUM_BANK, 0:CH])
            dve.tensor_copy(bqk[:, :], work[:, SUM_BANK, CH:CH + 1]).then_inc(wb_ready, 1)
            dve.wait_ge(wb_ready, 1)
            key_terms(0, range(TILES))
            key_bias(0)
            with dve.Fori(0, B - 1) as b:
                graph(b, True)
            graph(B - 1, False)

        @block.tensor
        def _(pe):
            def product(out_ps, lhs_hi, lhs_lo, rhs_hi, rhs_lo, first, last):
                pe.matmul(out_ps, lhs_hi, rhs_hi, start=first, stop=False)
                pe.matmul(out_ps, lhs_hi, rhs_lo, start=False, stop=False)
                return pe.matmul(out_ps, lhs_lo, rhs_hi, start=False, stop=last)

            def hidden(b, g):
                half, c = divmod(g, CH)
                for n in range(TPH):
                    last = pe.transpose(work[:, H_BANK[g], n * P:(n + 1) * P],
                                        xn[:, half * TPH + n, c * P:(c + 1) * P], ident[:, :])
                last.then_inc(hT_done, 1)

            def scores(b, u):
                if u < 2:
                    pe.wait_ge(v_lo_ready, TILES * b + V_BANK.index(u, TPH) + 1)
                else:
                    pe.wait_ge(exp_ready, UNITS * b + u - 1)
                half, i = divmod(u, TILES)
                keys = slice(i * P, (i + 1) * P)
                queries = slice(half * BANK, (half + 1) * BANK)
                for c in range(CH):
                    last = product(work[:, u % 2], uT_hi[:, c, keys], uT_lo[:, c, keys],
                                   hT_hi[:, c, queries], hT_lo[:, c, queries], c == 0, c == CH - 1)
                last.then_inc(scores_done, 1)

            def row_sums(b, half):
                pe.wait_ge(sum_ready, summed(b, TILES * (half + 1) - 1))
                for m in range(TPH):
                    n = half * TPH + m
                    last = pe.matmul(work[:, SUM_BANK, n:n + 1], prob_sum[:, m * P:(m + 1) * P], ones[:, :],
                                     start=True, stop=True)
                last.then_inc(row_sums_done, 1)

            def weighted_sum(b, u):
                half, i = divmod(u, TILES)
                pe.wait_ge(pT_lo_ready, UNITS * b + u + 1)
                if u == 0:
                    pe.wait_ge(v_lo_ready, TILES * b + TILES)
                for m in range(TPH):
                    if half and i == 0:
                        pe.wait_ge(out_ready, TILES * b + m + 1)
                    last = product(o_ps[:, m], pT_hi[:, u % RING, m * P:(m + 1) * P],
                                   pT_lo[:, u % RING, m * P:(m + 1) * P],
                                   v_hi[:, i], v_lo[:, i], i == 0, i == TILES - 1)
                    if i == TILES - 1:
                        last.then_inc(o_done, 1)

            def graph(b, following):
                for g in range(GROUPS):
                    half, c_out = divmod(g, CH)
                    if g < 3:
                        pe.wait_ge(hT_lo_ready, GROUPS * b + GROUPS - 2 + g)
                    elif g == 3:
                        pe.wait_ge(uT_lo_ready, GROUPS * b + 1)
                    else:
                        pe.wait_ge(uT_lo_ready, GROUPS * b + g - 3)
                    cols = slice(half * BANK, (half + 1) * BANK)
                    outs = slice(c_out * P, (c_out + 1) * P)
                    for c in range(CH):
                        last = product(work[:, U_BANK[g]], mT_hi[:, c, outs], mT_lo[:, c, outs],
                                       hT_hi[:, c, cols], hT_lo[:, c, cols], c == 0, c == CH - 1)
                    last.then_inc(uT_done, 1)
                for i in range(TILES):
                    if i < 4:
                        pe.wait_ge(uT_lo_ready, GROUPS * b + GROUPS - 3 + i)
                    else:
                        pe.wait_ge(v_lo_ready, TILES * b + i - 3)
                    rows = slice(i * P, (i + 1) * P)
                    for c in range(CH):
                        last = product(work[:, V_BANK[i]], hT_hi[:, c, rows], hT_lo[:, c, rows],
                                       wvT_hi[:, c], wvT_lo[:, c], c == 0, c == CH - 1)
                    last.then_inc(v_done, 1)
                for u in range(UNITS):
                    scores(b, u)
                    if u == TILES + 1:
                        row_sums(b, 0)
                    if u >= LAG:
                        weighted_sum(b, u - LAG)
                if following:
                    pe.wait_ge(xn_ready, TILES * (b + 1) + TILES)
                for g in range(GROUPS):
                    if following:
                        if g < 2:
                            pe.wait_ge(exp_ready, UNITS * b + UNITS - 1 + g)
                        elif g >= 3:
                            pe.wait_ge(hT_lo_ready, GROUPS * (b + 1) + g - 2)
                        hidden(b + 1, g)
                    if g in (2, 5):
                        weighted_sum(b, UNITS - LAG + g // 3)
                row_sums(b, 1)
                weighted_sum(b, UNITS - 1)

            for c in range(CH):
                pe.wait_ge(wqk_loaded[c], 32)
                for c_in in range(CH):
                    last = pe.matmul(work[:, c_in], wk_in[:, c, c_in * P:(c_in + 1) * P], wq_in[:, c],
                                     start=(c == 0), stop=(c == CH - 1))
            last.then_inc(mT_done, 1)
            pe.wait_ge(wv_loaded, 16)
            pe.wait_ge(consts_ready, 4)
            for c_in in range(CH):
                for c in range(CH):
                    last = pe.transpose(o_ps[:, c_in, c * P:(c + 1) * P], wv_in[:, c, c_in * P:(c_in + 1) * P],
                                        ident[:, :])
                last.then_inc(wvT_done, 1)
            pe.wait_ge(bq_rep_ready, 1)
            pe.wait_ge(w_lo_ready, CH + 1)
            for c_out in range(CH):
                for c in range(CH):
                    pe.matmul(work[:, SUM_BANK, c_out:c_out + 1], wq_in[:, c, c_out * P:(c_out + 1) * P],
                              bk_col[:, c:c + 1], start=(c == 0), stop=(c == CH - 1))
            for c in range(CH):
                pe.matmul(work[:, SUM_BANK, CH:CH + 1], bq_rep[:, c], bk_col[:, c:c + 1],
                          start=(c == 0), stop=(c == CH - 1))
            for c in range(CH):
                last = pe.matmul(o_ps[:, 0], bq_rep[:, c], wk_in[:, c], start=(c == 0), stop=(c == CH - 1))
            last.then_inc(wb_done, 1)
            pe.wait_ge(xn_ready, TILES)
            for g in range(GROUPS):
                if g >= 3:
                    pe.wait_ge(hT_lo_ready, g - 2)
                hidden(0, g)
            with pe.Fori(0, B - 1) as b:
                graph(b, True)
            graph(B - 1, False)


_INS = ['x', 'adj', 'L0_gnn_Wq_w', 'L0_gnn_Wq_b', 'L0_gnn_Wk_w', 'L0_gnn_Wk_b', 'L0_gnn_Wv_w', 'L0_gnn_Wv_b']


def kernel(**inputs):
    import numpy as _np
    import concourse.bacc as _bacc
    from concourse import mybir as _mybir
    from concourse.bass_utils import run_bass_kernel_spmd as _run

    nc = _bacc.Bacc("TRN2", target_bir_lowering=False, num_devices=1)
    arrays, args = {}, []
    for name in _INS:
        a = _np.ascontiguousarray(inputs[name])
        arrays[f"in_{name}_dram"] = a
        args.append(nc.dram_tensor(f"in_{name}_dram", a.shape, _mybir.dt.from_np(a.dtype), kind="ExternalInput").ap())
    shape = tuple(inputs['x'].shape)
    args.append(nc.dram_tensor("out_0_dram", shape, _mybir.dt.float32, kind="ExternalOutput").ap())
    adjacency_attention_kernel(nc, *args)
    r = _run(nc, [arrays], core_ids=[0])
    return r.results[0]["out_0_dram"]
```

```python
from contextlib import ExitStack

import concourse.bass as bass
from concourse import mybir



def adjacency_attention_kernel(nc, x, adj, wq, bq, wk, bk, wv, bv, out):
    ALU = mybir.AluOpType
    ACT = mybir.ActivationFunctionType
    AX = mybir.AxisListType
    F32 = mybir.dt.float32
    F32R = mybir.dt.float32r
    P = 128
    EPS = 1e-5
    B, N, D = x.shape
    BANK = 512
    TILES = N // P
    CH = D // P
    HALVES = N // BANK
    TPH = TILES // HALVES
    GROUPS = CH * HALVES
    UNITS = HALVES * TILES
    SQ = 32
    QUADS = P // SQ
    RING = 4
    LAG = 3
    assert D == BANK and HALVES == 2 and TPH == CH == QUADS == 4 and B % 2 == 0

    H_BANK = [(0, 1, 3)[g % 3] for g in range(GROUPS)]
    U_BANK = [(3, 0, 1, 2)[g % 4] for g in range(GROUPS)]
    V_BANK = U_BANK
    SUM_BANK = 2
    WV_BANK = (2, 3, 0, 1)

    x_rows = x.rearrange("b (M p m) d -> b p M (m d)", p=P, m=TPH)
    out_rows = out.rearrange("b (M p m) d -> b p M (m d)", p=P, m=TPH)
    adj_blocks = adj.rearrange("b (Q a c m) (K g j) -> b K g Q c m a j", Q=HALVES, a=QUADS, m=TPH, K=HALVES, g=QUADS)

    with ExitStack() as ctx:
        def sb(name, shape, dt=F32):
            return ctx.enter_context(nc.sbuf_tensor(name, shape, dt))

        def sem(name):
            return ctx.enter_context(nc.semaphore(name))

        mT_hi = sb("mT_hi", [P, CH, D], F32R)
        mT_lo = sb("mT_lo", [P, CH, D], F32R)
        wvT_hi = sb("wvT_hi", [P, CH, D], F32R)
        wvT_lo = sb("wvT_lo", [P, CH, D], F32R)
        hT_hi = sb("hT_hi", [P, CH, N], F32R)
        hT_lo = sb("hT_lo", [P, CH, N], F32R)
        uT_hi = sb("uT_hi", [P, CH, N], F32R)
        uT_lo = sb("uT_lo", [P, CH, N], F32R)
        v_hi = sb("v_hi", [P, TILES, D], F32R)
        v_lo = sb("v_lo", [P, TILES, D], F32R)
        pT_hi = sb("pT_hi", [P, RING, BANK], F32R)
        pT_lo = sb("pT_lo", [P, RING, BANK], F32R)
        xn = sb("xn", [P, TILES, D])
        res = sb("res", [P, TPH, D])
        adj_in = sb("adj_in", [P, HALVES, TILES * QUADS // 2, P])
        prob = sb("prob", [P, RING, BANK])
        e_sb = sb("e_sb", [P, 2, BANK])
        prob_sum = sb("prob_sum", [P, BANK])
        ident = sb("ident", [P, P])
        fold = sb("fold", [P, P])
        c_rep = sb("c_rep", [P, D])
        bv_rep = sb("bv_rep", [P, D])
        products = sb("products", [P, D])
        a_col = sb("a_col", [P, CH])
        bqk = sb("bqk", [P, 1])
        bq_col = sb("bq_col", [P, CH])
        bk_col = sb("bk_col", [P, CH])
        stats = sb("stats", [P, TILES, 6])
        mean_var = sb("mean_var", [P, TILES, 2])
        var_eps = sb("var_eps", [P, TILES])
        minus_half = sb("minus_half", [P, TILES])
        rstd = sb("rstd", [P, TILES])
        s_raw = sb("s_raw", [P, TILES])
        s_col = sb("s_col", [P, TILES])
        quad_sum = sb("quad_sum", [P, TILES * QUADS // 2])
        row_inv = sb("row_inv", [P, TILES])
        wk_in = adj_in[:, 0].rearrange("p (c e) q -> p c (e q)", c=CH)
        wq_in = adj_in[:, 1].rearrange("p (c e) q -> p c (e q)", c=CH)
        wv_in = res
        bq_rep = e_sb[:, 0].rearrange("p (c q) -> p c q", c=CH)

        work = ctx.enter_context(nc.psum_tensor("work", [P, 4, BANK], F32))
        o_ps = ctx.enter_context(nc.psum_tensor("o_ps", [P, TPH, BANK], F32))

        wqk_loaded = [sem(f"wqk{c}_loaded") for c in range(CH)]
        biases_loaded = sem("biases_loaded")
        wv_loaded = sem("wv_loaded")
        bv_loaded = sem("bv_loaded")
        x_loaded = [sem("x_half0_loaded"), sem("x_half1_loaded")]
        adj_loaded = [sem("adj_half0_loaded"), sem("adj_half1_loaded")]
        res_loaded = sem("res_loaded")
        out_stored = sem("out_stored")
        consts_ready = sem("consts_ready")
        rstd_ready = sem("rstd_ready")
        sum_ready = sem("sum_ready")
        res_bv_ready = sem("res_bv_ready")
        mT_done = sem("mT_done")
        wb_done = sem("wb_done")
        wvT_done = sem("wvT_done")
        hT_done = sem("hT_done")
        uT_done = sem("uT_done")
        v_done = sem("v_done")
        scores_done = sem("scores_done")
        row_sums_done = sem("row_sums_done")
        o_done = sem("o_done")
        w_hi_ready = sem("w_hi_ready")
        wb_ready = sem("wb_ready")
        hT_hi_ready = sem("hT_hi_ready")
        uT_hi_ready = sem("uT_hi_ready")
        v_hi_ready = sem("v_hi_ready")
        exp_ready = sem("exp_ready")
        pT_hi_ready = sem("pT_hi_ready")
        bq_rep_ready = sem("bq_rep_ready")
        w_lo_ready = sem("w_lo_ready")
        stats_done = sem("stats_done")
        mean_var_done = sem("mean_var_done")
        var_ready = sem("var_ready")
        xn_ready = sem("xn_ready")
        s_raw_done = sem("s_raw_done")
        s_ready = sem("s_ready")
        hT_lo_ready = sem("hT_lo_ready")
        uT_lo_ready = sem("uT_lo_ready")
        v_lo_ready = sem("v_lo_ready")
        adjT_ready = sem("adjT_ready")
        prob_ready = sem("prob_ready")
        pT_lo_ready = sem("pT_lo_ready")
        sumT_done = sem("sumT_done")
        quad_sum_ready = sem("quad_sum_ready")
        row_inv_ready = sem("row_inv_ready")
        out_ready = sem("out_ready")

        def summed(b, u):
            half, i = divmod(u, TILES)
            return (TILES - 1) * (HALVES * b + half) + max(i, 1)

        block = ctx.enter_context(nc.Block())

        @block.sync
        def _(sp):
            def load_x(b):
                for half in range(HALVES):
                    sp.dma_start(xn[:, half * TPH:(half + 1) * TPH], x_rows[b, :, half]
                                 .rearrange("p (m d) -> p m d", d=D)).then_inc(x_loaded[half], 16)

            def load_adj(b, n):
                queries, keys = divmod(n, HALVES)
                for g in range(QUADS):
                    sp.dma_start(adj_in[g * SQ:(g + 1) * SQ, keys].rearrange("c (m a) j -> c m a j", m=TPH),
                                 adj_blocks[b, keys, g, queries]).then_inc(adj_loaded[keys], 16)

            def load_res(b, half):
                sp.dma_start(res[:, :, :], x_rows[b, :, half].rearrange("p (m d) -> p m d", d=D)
                             ).then_inc(res_loaded, 16)

            def store_last_tiles():
                rows = out_rows[B - 1, :, HALVES - 1].rearrange("p (m d) -> p m d", d=D)
                for m in range(TPH):
                    sp.wait_ge(out_ready, TILES * B - TPH + m + 1)
                    sp.dma_start(rows[:, m], res[:, m]).then_inc(out_stored, 16)
                sp.wait_ge(out_stored, 16 * (HALVES * B - 1 + TPH))

            def store_out(b, half):
                sp.wait_ge(out_ready, TILES * b + TPH * (half + 1))
                sp.dma_start(out_rows[b, :, half].rearrange("p (m d) -> p m d", d=D), res[:, :, :]
                             ).then_inc(out_stored, 16)
                sp.wait_ge(out_stored, 16 * HALVES * b + 16 * (half + 1))

            def graph(b, following):
                if following:
                    sp.wait_ge(hT_done, GROUPS * b + GROUPS)
                    sp.wait_ge(s_raw_done, TILES * b + TILES)
                    load_x(b + 1)
                for n in range(2 * HALVES):
                    if n == HALVES + 1:
                        store_out(b, 0)
                        load_res(b, 1)
                    if n < HALVES or following:
                        sp.wait_ge(adjT_ready, UNITS * b + TPH * (n + 1))
                        if n < HALVES:
                            load_adj(b, n + HALVES)
                        else:
                            load_adj(b + 1, n - HALVES)
                if following:
                    store_out(b, 1)
                    load_res(b + 1, 0)
                else:
                    store_last_tiles()

            for c in range(CH):
                rows = slice(c * P, (c + 1) * P)
                sp.dma_start(wk_in[:, c], wk[rows, :]).then_inc(wqk_loaded[c], 16)
                sp.dma_start(wq_in[:, c], wq[rows, :]).then_inc(wqk_loaded[c], 16)
            sp.wait_ge(wb_done, 1)
            load_adj(0, 0)
            load_adj(0, 1)
            sp.wait_ge(wvT_done, CH)
            load_res(0, 0)
            with sp.Fori(0, B - 1) as b:
                graph(b, True)
            graph(B - 1, False)

        @block.gpsimd
        def _(pool):
            def reciprocal_std(b):
                pool.wait_ge(var_ready, b + 1)
                pool.tensor_tensor(rstd[:, :], var_eps[:, :], minus_half[:, :], ALU.pow).then_inc(rstd_ready, 1)

            def graph(b, following):
                for half in range(HALVES):
                    for i in range(TILES):
                        u = half * TILES + i
                        if i >= 2:
                            pool.wait_ge(sum_ready, summed(b, u - 1))
                        if u == TILES + 1:
                            pool.wait_ge(sumT_done, HALVES * b + 1)
                        if i >= 1:
                            before = prob[:, (u - 1) % RING] if i == 1 else prob_sum[:, :]
                            pool.wait_ge(prob_ready, UNITS * b + u + 1)
                            pool.tensor_tensor(prob_sum[:, :], before, prob[:, u % RING], ALU.add
                                               ).then_inc(sum_ready, 1)
                        if 2 <= i < 2 + TPH:
                            m = i - 2
                            if m == 0:
                                pool.wait_ge(res_loaded, 16 * HALVES * b + 16 * (half + 1))
                            pool.tensor_tensor(res[:, m], res[:, m], bv_rep[:, :], ALU.add
                                               ).then_inc(res_bv_ready, 1)
                        if following and u == TPH + 3:
                            reciprocal_std(b + 1)

            pool.memset(ident[:, :], 0.0).then_inc(consts_ready, 1)
            pool.memset(minus_half[:, :], -0.5).then_inc(consts_ready, 1)
            pool.memset(fold[:, :], 0.0).then_inc(consts_ready, 1)
            pool.wait_ge(consts_ready, 3)
            pool.affine_select(out=ident[:, :], in_=ident[:, :], compare_op=ALU.not_equal, fill=1.0,
                               base=0, pattern=[[-1, P]], channel_multiplier=1).then_inc(consts_ready, 1)
            fold_blocks = fold[:, :].rearrange("p (a r) -> p a r", r=SQ)
            for a in range(QUADS):
                pool.affine_select(out=fold_blocks, in_=fold_blocks, compare_op=ALU.not_equal, fill=1.0,
                                   base=-a * SQ, pattern=[[0, QUADS], [-1, SQ]], channel_multiplier=1
                                   ).then_inc(consts_ready, 1)
                pool.wait_ge(consts_ready, 5 + a)
            reciprocal_std(0)
            pool.wait_ge(bv_loaded, 16)
            with pool.Fori(0, B - 1) as b:
                graph(b, True)
            graph(B - 1, False)

        @block.scalar
        def _(act):
            def hidden_hi(b, g):
                act.wait_ge(hT_done, GROUPS * b + g + 1)
                half, c = divmod(g, CH)
                act.activation(hT_hi[:, c, half * BANK:(half + 1) * BANK], work[:, H_BANK[g]], ACT.Relu
                               ).then_inc(hT_hi_ready, 1)

            def graph(b, following):
                for i in range(TILES):
                    act.wait_ge(v_done, TILES * b + i + 1)
                    act.activation(v_hi[:, i], work[:, V_BANK[i]], ACT.Copy).then_inc(v_hi_ready, 1)
                for g in range(GROUPS):
                    act.wait_ge(uT_done, GROUPS * b + g + 1)
                    half, c = divmod(g, CH)
                    act.activation(uT_hi[:, c, half * BANK:(half + 1) * BANK], work[:, U_BANK[g]], ACT.Identity,
                                   bias=a_col[:, c:c + 1]).then_inc(uT_hi_ready, 1)
                act.wait_ge(s_ready, b + 1)
                for u in range(UNITS):
                    i = u % TILES
                    if u >= 2:
                        act.wait_ge(prob_ready, UNITS * b + u - 1)
                    act.wait_ge(scores_done, UNITS * b + u + 1)
                    act.activation(e_sb[:, u % 2], work[:, u % 2], ACT.Exp, bias=s_col[:, i:i + 1]
                                   ).then_inc(exp_ready, 1)
                    act.wait_ge(prob_ready, UNITS * b + u + 1)
                    act.activation(pT_hi[:, u % RING], prob[:, u % RING], ACT.Copy).then_inc(pT_hi_ready, 1)
                if following:
                    for g in range(GROUPS):
                        hidden_hi(b + 1, g)

            act.dma_start(bk_col[:, :], bk.rearrange("(c p) -> p c", p=P), allow_slow_non_contiguous=True
                          ).then_inc(biases_loaded, 16)
            act.dma_start(bq_col[:, :], bq.rearrange("(c p) -> p c", p=P), allow_slow_non_contiguous=True
                          ).then_inc(biases_loaded, 16)
            for half in range(HALVES):
                act.dma_start(xn[:, half * TPH:(half + 1) * TPH],
                              x_rows[0, :, half].rearrange("p (m d) -> p m d", d=D)).then_inc(x_loaded[half], 16)
            act.dma_start(wv_in[:, :, :], wv.rearrange("(c p) d -> p c d", p=P)).then_inc(wv_loaded, 16)
            act.dma_start(bv_rep[:, :], bv.rearrange("(a d) -> a d", a=1).partition_broadcast(P)
                          ).then_inc(bv_loaded, 16)
            act.wait_ge(mT_done, 1)
            for c in range(CH):
                act.activation(mT_hi[:, c], work[:, c], ACT.Copy).then_inc(w_hi_ready, 1)
            act.wait_ge(wb_done, 1)
            act.activation(c_rep[:, :], o_ps[:, 0], ACT.Copy)
            act.activation(a_col[:, :], o_ps[:, 1, 0:CH], ACT.Copy)
            act.activation(bqk[:, :], o_ps[:, 1, CH:CH + 1], ACT.Copy).then_inc(wb_ready, 1)
            for c in range(CH):
                act.wait_ge(wvT_done, c + 1)
                act.activation(wvT_hi[:, c], o_ps[:, WV_BANK[c]], ACT.Copy).then_inc(w_hi_ready, 1)
            for g in range(GROUPS):
                hidden_hi(0, g)
            act.wait_ge(wb_ready, 1)
            with act.Fori(0, B - 1) as b:
                graph(b, True)
            graph(B - 1, False)

        @block.vector
        def _(dve):
            def row_stats(tiles):
                for i in tiles:
                    dve.bn_stats(stats[:, i], xn[:, i]).then_inc(stats_done, 1)

            def mean_and_variance(tiles):
                for i in tiles:
                    dve.bn_aggr(mean_var[:, i], stats[:, i]).then_inc(mean_var_done, 1)

            def variance(b):
                dve.wait_ge(mean_var_done, TILES * b + TILES)
                dve.tensor_scalar(var_eps[:, :], mean_var[:, :, 1], EPS, None, ALU.add).then_inc(var_ready, 1)

            def normalise(tiles):
                for i in tiles:
                    dve.tensor_scalar(xn[:, i], xn[:, i], mean_var[:, i, 0:1], rstd[:, i:i + 1],
                                      ALU.subtract, ALU.mult).then_inc(xn_ready, 1)

            def key_terms(b, tiles):
                for i in tiles:
                    dve.wait_ge(xn_ready, TILES * b + i + 1)
                    if not (isinstance(b, int) and b == i == 0):
                        dve.wait_ge(s_raw_done, TILES * b + i)
                    dve.scalar_tensor_tensor(out=products[:, :], in0=xn[:, i], scalar=0.0, in1=c_rep[:, :],
                                             op0=ALU.max, op1=ALU.mult, accum_out=s_raw[:, i:i + 1]
                                             ).then_inc(s_raw_done, 1)

            def key_bias(b):
                dve.wait_ge(s_raw_done, TILES * b + TILES)
                dve.tensor_scalar(s_col[:, :], s_raw[:, :], bqk[:, 0:1], None, ALU.add).then_inc(s_ready, 1)

            def hidden_lo(b, g):
                dve.wait_ge(hT_hi_ready, GROUPS * b + g + 1)
                half, c = divmod(g, CH)
                cols = slice(half * BANK, (half + 1) * BANK)
                dve.scalar_tensor_tensor(out=hT_lo[:, c, cols], in0=work[:, H_BANK[g]], scalar=0.0,
                                         in1=hT_hi[:, c, cols].bitcast(F32), op0=ALU.max, op1=ALU.subtract
                                         ).then_inc(hT_lo_ready, 1)

            def transpose_adj(b, u):
                queries, i = divmod(u, TILES)
                keys, m = divmod(i, TPH)
                if m == 0:
                    dve.wait_ge(adj_loaded[keys], 16 * QUADS * (HALVES * b + queries + 1))
                if u >= RING:
                    dve.wait_ge(sum_ready, summed(b, u - RING))
                    dve.wait_ge(pT_lo_ready, UNITS * b + u - RING + 1)
                dve.transpose(prob[:, u % RING].rearrange("p (n c) -> p n c", c=SQ),
                              adj_in[:, keys].rearrange("p n (r m) -> p n r m", m=TPH)[:, :, :, m]
                              ).then_inc(adjT_ready, 1)

            def quadrant_sums(b, half):
                dve.wait_ge(sum_ready, summed(b, TILES * (half + 1) - 1))
                dve.transpose(products[:, :].rearrange("p (n c) -> p n c", c=SQ),
                              prob_sum[:, :].rearrange("p (n r) -> p n r", r=SQ)).then_inc(sumT_done, 1)
                dve.wait_ge(sumT_done, HALVES * b + half + 1)
                dve.reduce_sum(quad_sum[:, :], products[:, :].rearrange("p (n c) -> p n c", c=SQ), axis=AX.X
                               ).then_inc(quad_sum_ready, 1)

            def results(b, half):
                dve.wait_ge(row_sums_done, HALVES * b + half + 1)
                sums = work[:, SUM_BANK, half * BANK // 2:half * BANK // 2 + TPH * QUADS].rearrange(
                    "p (m a) -> p m a", a=QUADS)
                for a in range(QUADS):
                    rows = slice(a * SQ, (a + 1) * SQ)
                    last = dve.reciprocal(row_inv[rows, half * TPH:(half + 1) * TPH], sums[rows, :, a])
                last.then_inc(row_inv_ready, 1)
                dve.wait_ge(row_inv_ready, HALVES * b + half + 1)
                for m in range(TPH):
                    n = half * TPH + m
                    dve.wait_ge(res_bv_ready, TILES * b + n + 1)
                    dve.wait_ge(o_done, TILES * b + n + 1)
                    dve.scalar_tensor_tensor(out=res[:, m], in0=o_ps[:, m], scalar=row_inv[:, n:n + 1],
                                             in1=res[:, m], op0=ALU.mult, op1=ALU.add).then_inc(out_ready, 1)

            def graph(b, following):
                for i in range(TILES):
                    dve.wait_ge(v_hi_ready, TILES * b + i + 1)
                    dve.tensor_tensor(v_lo[:, i], work[:, V_BANK[i]], v_hi[:, i].bitcast(F32),
                                      ALU.subtract).then_inc(v_lo_ready, 1)
                for g in range(GROUPS):
                    dve.wait_ge(uT_hi_ready, GROUPS * b + g + 1)
                    half, c = divmod(g, CH)
                    cols = slice(half * BANK, (half + 1) * BANK)
                    dve.scalar_tensor_tensor(out=uT_lo[:, c, cols], in0=work[:, U_BANK[g]],
                                             scalar=a_col[:, c:c + 1], in1=uT_hi[:, c, cols].bitcast(F32),
                                             op0=ALU.add, op1=ALU.subtract).then_inc(uT_lo_ready, 1)
                    if g < 2:
                        transpose_adj(b, g)
                for u in range(UNITS):
                    dve.wait_ge(exp_ready, UNITS * b + u + 1)
                    dve.wait_ge(adjT_ready, UNITS * b + u + 1)
                    dve.tensor_tensor(prob[:, u % RING], e_sb[:, u % 2], prob[:, u % RING], ALU.mult
                                      ).then_inc(prob_ready, 1)
                    if u + 2 < UNITS:
                        transpose_adj(b, u + 2)
                    aggregated = following and 2 <= u <= TILES // 2 + 1
                    if aggregated:
                        dve.wait_ge(stats_done, TILES * (b + 1) + 2 * u - 2)
                    if following and u == TILES:
                        dve.wait_ge(rstd_ready, b + 2)
                    dve.wait_ge(pT_hi_ready, UNITS * b + u + 1)
                    dve.tensor_tensor(pT_lo[:, u % RING], prob[:, u % RING], pT_hi[:, u % RING].bitcast(F32),
                                      ALU.subtract).then_inc(pT_lo_ready, 1)
                    if following:
                        if aggregated:
                            mean_and_variance([2 * u - 4, 2 * u - 3])
                        if u in (1, TPH // 2 + 1):
                            dve.wait_ge(x_loaded[u // 2], 16 * b + 32)
                        if 1 <= u <= TILES // 2:
                            row_stats([2 * u - 2, 2 * u - 1])
                        if u == TILES // 2 + 1:
                            variance(b + 1)
                        if u in (TILES, TILES + 1):
                            normalise(range((u - TILES) * TPH, (u - TILES + 1) * TPH))
                        if TILES + LAG <= u < TILES + LAG + 4:
                            key_terms(b + 1, [2 * (u - TILES - LAG), 2 * (u - TILES - LAG) + 1])
                    if u == TILES:
                        quadrant_sums(b, 0)
                    if u == TILES + LAG - 1:
                        results(b, 0)
                if following:
                    for g in range(3):
                        hidden_lo(b + 1, g)
                    dve.wait_ge(s_raw_done, TILES * (b + 1) + TILES)
                quadrant_sums(b, 1)
                if following:
                    for g in range(3, GROUPS):
                        hidden_lo(b + 1, g)
                    key_bias(b + 1)
                results(b, 1)

            dve.wait_ge(biases_loaded, 32)
            for c in range(CH):
                last = dve.tensor_copy(bq_rep[:, c], bq_col[:, c:c + 1].broadcast_to([P, P]))
            last.then_inc(bq_rep_ready, 1)
            for half in range(HALVES):
                dve.wait_ge(x_loaded[half], 16)
                row_stats(range(half * TPH, (half + 1) * TPH))
            dve.wait_ge(stats_done, TILES)
            mean_and_variance(range(TILES))
            variance(0)
            for c in range(CH):
                dve.wait_ge(w_hi_ready, c + 1)
                dve.tensor_tensor(mT_lo[:, c], work[:, c], mT_hi[:, c].bitcast(F32), ALU.subtract
                                  ).then_inc(w_lo_ready, 1)
            dve.wait_ge(rstd_ready, 1)
            normalise(range(TILES))
            for c in range(CH):
                dve.wait_ge(w_hi_ready, CH + c + 1)
                dve.tensor_tensor(wvT_lo[:, c], o_ps[:, WV_BANK[c]], wvT_hi[:, c].bitcast(F32), ALU.subtract
                                  ).then_inc(w_lo_ready, 1)
            for g in range(GROUPS):
                hidden_lo(0, g)
            dve.wait_ge(wb_ready, 1)
            key_terms(0, range(TILES))
            key_bias(0)
            with dve.Fori(0, B - 1) as b:
                graph(b, True)
            graph(B - 1, False)

        @block.tensor
        def _(pe):
            def product(out_ps, lhs_hi, lhs_lo, rhs_hi, rhs_lo, first, last):
                pe.matmul(out_ps, lhs_hi, rhs_hi, start=first, stop=False)
                pe.matmul(out_ps, lhs_hi, rhs_lo, start=False, stop=False)
                return pe.matmul(out_ps, lhs_lo, rhs_hi, start=False, stop=last)

            def hidden(b, g):
                half, c = divmod(g, CH)
                for n in range(TPH):
                    last = pe.transpose(work[:, H_BANK[g], n * P:(n + 1) * P],
                                        xn[:, half * TPH + n, c * P:(c + 1) * P], ident[:, :])
                last.then_inc(hT_done, 1)

            def scores(b, u):
                if u < 2:
                    pe.wait_ge(uT_lo_ready, GROUPS * b + U_BANK.index(u, 4) + 1)
                else:
                    pe.wait_ge(exp_ready, UNITS * b + u - 1)
                half, i = divmod(u, TILES)
                if u == TPH:
                    pe.wait_ge(uT_lo_ready, GROUPS * b + GROUPS)
                keys = slice(i * P, (i + 1) * P)
                queries = slice(half * BANK, (half + 1) * BANK)
                for c in range(CH):
                    last = product(work[:, u % 2], uT_hi[:, c, keys], uT_lo[:, c, keys],
                                   hT_hi[:, c, queries], hT_lo[:, c, queries], c == 0, c == CH - 1)
                last.then_inc(scores_done, 1)

            def row_sums(b, half):
                pe.wait_ge(quad_sum_ready, HALVES * b + half + 1)
                at = half * BANK // 2
                pe.matmul(work[:, SUM_BANK, at:at + TPH * QUADS], fold[:, :], quad_sum[:, :],
                          start=True, stop=True).then_inc(row_sums_done, 1)

            def weighted_sum(b, u):
                half, i = divmod(u, TILES)
                pe.wait_ge(pT_lo_ready, UNITS * b + u + 1)
                for m in range(TPH):
                    if half and i == 0:
                        pe.wait_ge(out_ready, TILES * b + m + 1)
                    last = product(o_ps[:, m], pT_hi[:, u % RING, m * P:(m + 1) * P],
                                   pT_lo[:, u % RING, m * P:(m + 1) * P],
                                   v_hi[:, i], v_lo[:, i], i == 0, i == TILES - 1)
                    if i == TILES - 1:
                        last.then_inc(o_done, 1)

            def graph(b, following):
                for i in range(TILES):
                    if i < 3:
                        pe.wait_ge(hT_lo_ready, GROUPS * b + GROUPS - 2 + i)
                    elif i == 3:
                        pe.wait_ge(v_lo_ready, TILES * b + 1)
                    else:
                        pe.wait_ge(v_lo_ready, TILES * b + i - 3)
                    rows = slice(i * P, (i + 1) * P)
                    for c in range(CH):
                        last = product(work[:, V_BANK[i]], hT_hi[:, c, rows], hT_lo[:, c, rows],
                                       wvT_hi[:, c], wvT_lo[:, c], c == 0, c == CH - 1)
                    last.then_inc(v_done, 1)
                for g in range(GROUPS):
                    half, c_out = divmod(g, CH)
                    if g < 4:
                        pe.wait_ge(v_lo_ready, TILES * b + TILES - 3 + g)
                    else:
                        pe.wait_ge(uT_lo_ready, GROUPS * b + g - 3)
                    cols = slice(half * BANK, (half + 1) * BANK)
                    outs = slice(c_out * P, (c_out + 1) * P)
                    for c in range(CH):
                        last = product(work[:, U_BANK[g]], mT_hi[:, c, outs], mT_lo[:, c, outs],
                                       hT_hi[:, c, cols], hT_lo[:, c, cols], c == 0, c == CH - 1)
                    last.then_inc(uT_done, 1)
                for u in range(UNITS):
                    scores(b, u)
                    if u == TILES + 2:
                        row_sums(b, 0)
                    if u >= LAG:
                        weighted_sum(b, u - LAG)
                if following:
                    pe.wait_ge(xn_ready, TILES * (b + 1) + TILES)
                for g in range(GROUPS):
                    if following:
                        if g < 2:
                            pe.wait_ge(exp_ready, UNITS * b + UNITS - 1 + g)
                        elif g >= 3:
                            pe.wait_ge(hT_lo_ready, GROUPS * (b + 1) + g - 2)
                        hidden(b + 1, g)
                    if g in (2, 5):
                        weighted_sum(b, UNITS - LAG + g // 3)
                row_sums(b, 1)
                weighted_sum(b, UNITS - 1)

            for c in range(CH):
                pe.wait_ge(wqk_loaded[c], 32)
                for c_in in range(CH):
                    last = pe.matmul(work[:, c_in], wk_in[:, c, c_in * P:(c_in + 1) * P], wq_in[:, c],
                                     start=(c == 0), stop=(c == CH - 1))
                if c == CH - 1:
                    last.then_inc(mT_done, 1)
                if c == 0:
                    pe.wait_ge(bq_rep_ready, 1)
                pe.matmul(o_ps[:, 0], bq_rep[:, c], wk_in[:, c], start=(c == 0), stop=(c == CH - 1))
            for c_out in range(CH):
                for c in range(CH):
                    pe.matmul(o_ps[:, 1, c_out:c_out + 1], wq_in[:, c, c_out * P:(c_out + 1) * P],
                              bk_col[:, c:c + 1], start=(c == 0), stop=(c == CH - 1))
            for c in range(CH):
                last = pe.matmul(o_ps[:, 1, CH:CH + 1], bq_rep[:, c], bk_col[:, c:c + 1],
                                 start=(c == 0), stop=(c == CH - 1))
            last.then_inc(wb_done, 1)
            pe.wait_ge(wv_loaded, 16)
            pe.wait_ge(consts_ready, 8)
            for c_in in range(CH):
                if c_in == 2:
                    pe.wait_ge(wb_ready, 1)
                for c in range(CH):
                    last = pe.transpose(o_ps[:, WV_BANK[c_in], c * P:(c + 1) * P],
                                        wv_in[:, c, c_in * P:(c_in + 1) * P], ident[:, :])
                last.then_inc(wvT_done, 1)
            pe.wait_ge(w_lo_ready, CH)
            pe.wait_ge(xn_ready, TILES)
            for g in range(GROUPS):
                if g >= 3:
                    pe.wait_ge(hT_lo_ready, g - 2)
                hidden(0, g)
            with pe.Fori(0, B - 1) as b:
                graph(b, True)
            graph(B - 1, False)


_INS = ['x', 'adj', 'L0_gnn_Wq_w', 'L0_gnn_Wq_b', 'L0_gnn_Wk_w', 'L0_gnn_Wk_b', 'L0_gnn_Wv_w', 'L0_gnn_Wv_b']


def kernel(**inputs):
    import numpy as _np
    import concourse.bacc as _bacc
    from concourse import mybir as _mybir
    from concourse.bass_utils import run_bass_kernel_spmd as _run

    nc = _bacc.Bacc("TRN2", target_bir_lowering=False, num_devices=1)
    arrays, args = {}, []
    for name in _INS:
        a = _np.ascontiguousarray(inputs[name])
        arrays[f"in_{name}_dram"] = a
        args.append(nc.dram_tensor(f"in_{name}_dram", a.shape, _mybir.dt.from_np(a.dtype), kind="ExternalInput").ap())
    shape = tuple(inputs['x'].shape)
    args.append(nc.dram_tensor("out_0_dram", shape, _mybir.dt.float32, kind="ExternalOutput").ap())
    adjacency_attention_kernel(nc, *args)
    r = _run(nc, [arrays], core_ids=[0])
    return r.results[0]["out_0_dram"]
```

```python
from contextlib import ExitStack

import concourse.bass as bass
from concourse import mybir



def adjacency_attention_kernel(nc, x, adj, wq, bq, wk, bk, wv, bv, out):
    ALU = mybir.AluOpType
    ACT = mybir.ActivationFunctionType
    AX = mybir.AxisListType
    F32 = mybir.dt.float32
    F32R = mybir.dt.float32r
    P = 128
    EPS = 1e-5
    B, N, D = x.shape
    BANK = 512
    TILES = N // P
    CH = D // P
    HALVES = N // BANK
    TPH = TILES // HALVES
    GROUPS = CH * HALVES
    UNITS = HALVES * TILES
    SQ = 32
    QUADS = P // SQ
    RING = 4
    LAG = 3
    assert D == BANK and HALVES == 2 and TPH == CH == QUADS == 4 and B % 2 == 0

    BLOCKS = TILES * QUADS
    BPH = BLOCKS // HALVES
    BY_VECTOR = 10
    NORMALISED = (9, 11, 12, 13)

    U_BANK = [(3, 0, 1, 2)[g % 4] for g in range(GROUPS)]
    V_BANK = U_BANK
    SUM_BANK = 2
    MEAN_AT, VAR_AT = 64, 128
    WV_BANK = (0, 1, 2, 0)
    SUM_BANK_0 = 3
    C_BANK, A_BANK = 1, 2

    x_blocks = x.rearrange("b (M a c m) (g j) -> b M g c m a j", M=HALVES, a=QUADS, m=TPH, g=QUADS)
    x_rows = x.rearrange("b (M p m) d -> b p M (m d)", p=P, m=TPH)
    out_rows = out.rearrange("b (M p m) d -> b p M (m d)", p=P, m=TPH)
    adj_blocks = adj.rearrange("b (Q a c m) (K g j) -> b K g Q c m a j", Q=HALVES, a=QUADS, m=TPH, K=HALVES, g=QUADS)

    with ExitStack() as ctx:
        def sb(name, shape, dt=F32):
            return ctx.enter_context(nc.sbuf_tensor(name, shape, dt))

        def sem(name):
            return ctx.enter_context(nc.semaphore(name))

        mT_hi = sb("mT_hi", [P, CH, D], F32R)
        mT_lo = sb("mT_lo", [P, CH, D], F32R)
        wvT_hi = sb("wvT_hi", [P, CH, D], F32R)
        wvT_lo = sb("wvT_lo", [P, CH, D], F32R)
        hT_hi = sb("hT_hi", [P, CH, N], F32R)
        hT_lo = sb("hT_lo", [P, CH, N], F32R)
        uT_hi = sb("uT_hi", [P, CH, N], F32R)
        uT_lo = sb("uT_lo", [P, CH, N], F32R)
        v_hi = sb("v_hi", [P, TILES, D], F32R)
        v_lo = sb("v_lo", [P, TILES, D], F32R)
        pT_hi = sb("pT_hi", [P, RING, BANK], F32R)
        pT_lo = sb("pT_lo", [P, RING, BANK], F32R)
        xn = sb("xn", [P, BLOCKS, P])
        res = sb("res", [P, TPH, D])
        adj_in = sb("adj_in", [P, HALVES, TILES * QUADS // 2, P])
        prob = sb("prob", [P, RING, BANK])
        e_sb = sb("e_sb", [P, 2, BANK])
        prob_sum = sb("prob_sum", [P, BANK])
        ident = sb("ident", [P, P])
        fold = sb("fold", [P, P])
        c_block = sb("c_block", [P, P])
        bv_rep = sb("bv_rep", [P, D])
        spare = sb("spare", [P, BANK])
        a_col = sb("a_col", [P, CH])
        bqk = sb("bqk", [P, 1])
        bq_col = sb("bq_col", [P, CH])
        bk_col = sb("bk_col", [P, CH])
        stats = sb("stats", [P, BLOCKS, 2, 3])
        means, squares = stats[:, :, :, 1], stats[:, :, :, 2]
        block_sum = sb("block_sum", [P, BLOCKS])
        mean = sb("mean", [P, BLOCKS])
        dev = sb("dev", [P, BLOCKS, 2])
        dev_sq = sb("dev_sq", [P, BLOCKS, 2])
        var_eps = sb("var_eps", [P, BLOCKS])
        minus_half = sb("minus_half", [P, BLOCKS])
        rstd = sb("rstd", [P, BLOCKS])
        s_block = sb("s_block", [P, BLOCKS])
        s_col = sb("s_col", [P, TILES])
        quad_sum = sb("quad_sum", [P, TILES * QUADS // 2])
        row_inv = sb("row_inv", [P, TILES])
        wk_in = adj_in[:, 0].rearrange("p (c e) q -> p c (e q)", c=CH)
        wq_in = adj_in[:, 1].rearrange("p (c e) q -> p c (e q)", c=CH)
        wv_in = res
        bq_rep = e_sb[:, 0].rearrange("p (c r) -> p c r", c=CH)
        wq_bk = e_sb[:, 1]
        bk_rows = (spare[:, :], prob_sum[:, :], prob[:, 2], prob[:, 3])
        mT_full = (e_sb[:, 0], e_sb[:, 1], prob_sum[:, :], spare[:, :])
        ones = c_block

        work = ctx.enter_context(nc.psum_tensor("work", [P, 4, BANK], F32))
        o_ps = ctx.enter_context(nc.psum_tensor("o_ps", [P, TPH, BANK], F32))

        wqk_loaded = [sem(f"wqk{c}_loaded") for c in range(CH)]
        biases_loaded = sem("biases_loaded")
        wv_loaded = sem("wv_loaded")
        bv_loaded = sem("bv_loaded")
        x_loaded = [sem("x_half0_loaded"), sem("x_half1_loaded")]
        adj_loaded = [sem("adj_half0_loaded"), sem("adj_half1_loaded")]
        res_loaded = sem("res_loaded")
        out_stored = sem("out_stored")
        consts_ready = sem("consts_ready")
        mT_lo_ready = sem("mT_lo_ready")
        wq_bk_ready = sem("wq_bk_ready")
        rstd_ready = sem("rstd_ready")
        sum_ready = sem("sum_ready")
        res_bv_ready = sem("res_bv_ready")
        mT_done = sem("mT_done")
        wb_done = sem("wb_done")
        wvT_done = sem("wvT_done")
        mean_done = sem("mean_done")
        var_done = sem("var_done")
        s_done = sem("s_done")
        uT_done = sem("uT_done")
        v_done = sem("v_done")
        scores_done = sem("scores_done")
        row_sums_done = sem("row_sums_done")
        o_done = sem("o_done")
        bk_rows_ready = sem("bk_rows_ready")
        wvT_hi_ready = sem("wvT_hi_ready")
        mT_hi_ready = sem("mT_hi_ready")
        wb_ready = sem("wb_ready")
        hT_hi_ready = sem("hT_hi_ready")
        uT_hi_ready = sem("uT_hi_ready")
        v_hi_ready = sem("v_hi_ready")
        exp_ready = sem("exp_ready")
        pT_hi_ready = sem("pT_hi_ready")
        bq_rep_ready = sem("bq_rep_ready")
        wvT_lo_ready = sem("wvT_lo_ready")
        stats_done = sem("stats_done")
        mean_sum_ready = sem("mean_sum_ready")
        var_step_done = sem("var_step_done")
        var_sum_ready = sem("var_sum_ready")
        var_ready = sem("var_ready")
        xn_ready = sem("xn_ready")
        xnT_ready = sem("xnT_ready")
        s_block_ready = sem("s_block_ready")
        s_ready = sem("s_ready")
        hT_lo_ready = sem("hT_lo_ready")
        uT_lo_ready = sem("uT_lo_ready")
        v_lo_ready = sem("v_lo_ready")
        adjT_ready = sem("adjT_ready")
        prob_ready = sem("prob_ready")
        pT_lo_ready = sem("pT_lo_ready")
        sumT_done = sem("sumT_done")
        quad_sum_ready = sem("quad_sum_ready")
        row_inv_ready = sem("row_inv_ready")
        out_ready = sem("out_ready")

        def summed(b, u):
            half, i = divmod(u, TILES)
            return (TILES - 1) * (HALVES * b + half) + max(i, 1)

        def norm_no(b, half=None):
            return b + HALVES if half is None else half + 1

        def norm_blocks(half=None):
            return slice(0, BLOCKS) if half is None else slice(half * BPH, (half + 1) * BPH)

        def xnT(b, g):
            if g < CH and not (isinstance(b, int) and b == 0):
                return spare[:, :]
            return prob[:, g % RING]

        block = ctx.enter_context(nc.Block())

        def load_first_x(queue, half, g):
            queue.dma_start(xn[g * SQ:(g + 1) * SQ, half * BPH:(half + 1) * BPH]
                            .rearrange("c (m a) j -> c m a j", m=TPH),
                            x_blocks[0, half, g]).then_inc(x_loaded[half], 16)

        @block.sync
        def _(sp):
            def load_x(b):
                for half in range(HALVES):
                    for g in range(QUADS):
                        sp.dma_start(xn[g * SQ:(g + 1) * SQ, half * BPH:(half + 1) * BPH]
                                     .rearrange("c (m a) j -> c m a j", m=TPH),
                                     x_blocks[b, half, g]).then_inc(x_loaded[half], 16)

            def load_adj(b, n):
                queries, keys = divmod(n, HALVES)
                for g in range(QUADS):
                    sp.dma_start(adj_in[g * SQ:(g + 1) * SQ, keys].rearrange("c (m a) j -> c m a j", m=TPH),
                                 adj_blocks[b, keys, g, queries]).then_inc(adj_loaded[keys], 16)

            def load_res(b, half):
                sp.dma_start(res[:, :, :], x_rows[b, :, half].rearrange("p (m d) -> p m d", d=D)
                             ).then_inc(res_loaded, 16)

            def store_last_tiles():
                rows = out_rows[B - 1, :, HALVES - 1].rearrange("p (m d) -> p m d", d=D)
                for m in range(TPH):
                    sp.wait_ge(out_ready, TILES * B - TPH + m + 1)
                    sp.dma_start(rows[:, m], res[:, m]).then_inc(out_stored, 16)
                sp.wait_ge(out_stored, 16 * (HALVES * B - 1 + TPH))

            def store_out(b, half):
                sp.wait_ge(out_ready, TILES * b + TPH * (half + 1))
                sp.dma_start(out_rows[b, :, half].rearrange("p (m d) -> p m d", d=D), res[:, :, :]
                             ).then_inc(out_stored, 16)
                sp.wait_ge(out_stored, 16 * HALVES * b + 16 * (half + 1))

            def graph(b, following):
                if following:
                    sp.wait_ge(xnT_ready, GROUPS * b + GROUPS)
                    sp.wait_ge(s_block_ready, BLOCKS * b + BLOCKS)
                    load_x(b + 1)
                for n in range(2 * HALVES):
                    if n == HALVES + 1:
                        store_out(b, 0)
                        load_res(b, 1)
                    if n < HALVES or following:
                        sp.wait_ge(adjT_ready, UNITS * b + TPH * (n + 1))
                        if n < HALVES:
                            load_adj(b, n + HALVES)
                        else:
                            load_adj(b + 1, n - HALVES)
                if following:
                    store_out(b, 1)
                    load_res(b + 1, 0)
                else:
                    store_last_tiles()

            for c in range(CH):
                rows = slice(c * P, (c + 1) * P)
                sp.dma_start(wk_in[:, c], wk[rows, :]).then_inc(wqk_loaded[c], 16)
                sp.dma_start(wq_in[:, c], wq[rows, :]).then_inc(wqk_loaded[c], 16)
                if c == 0:
                    for g in range(2, QUADS):
                        load_first_x(sp, 0, g)
            sp.wait_ge(wb_done, 1)
            sp.wait_ge(mT_done, 1)
            load_adj(0, 0)
            load_adj(0, 1)
            sp.wait_ge(wvT_done, CH)
            load_res(0, 0)
            with sp.Fori(0, B - 1) as b:
                graph(b, True)
            graph(B - 1, False)

        @block.gpsimd
        def _(pool):
            def reciprocal_std(b, half=None):
                pool.wait_ge(var_ready, norm_no(b, half))
                cols = norm_blocks(half)
                pool.tensor_tensor(rstd[:, cols], var_eps[:, cols], minus_half[:, cols], ALU.pow
                                   ).then_inc(rstd_ready, 1)

            def graph(b, following):
                for half in range(HALVES):
                    for i in range(TILES):
                        u = half * TILES + i
                        if i >= 2:
                            pool.wait_ge(sum_ready, summed(b, u - 1))
                        if u == TILES + 1:
                            pool.wait_ge(sumT_done, HALVES * b + 1)
                        if i >= 1:
                            before = prob[:, (u - 1) % RING] if i == 1 else prob_sum[:, :]
                            pool.wait_ge(prob_ready, UNITS * b + u + 1)
                            pool.tensor_tensor(prob_sum[:, :], before, prob[:, u % RING], ALU.add
                                               ).then_inc(sum_ready, 1)
                        if 2 <= i < 2 + TPH:
                            m = i - 2
                            if m == 0:
                                pool.wait_ge(res_loaded, 16 * HALVES * b + 16 * (half + 1))
                            pool.tensor_tensor(res[:, m], res[:, m], bv_rep[:, :], ALU.add
                                               ).then_inc(res_bv_ready, 1)
                        if following and u == TILES:
                            reciprocal_std(b + 1)

            pool.memset(ones[:, :], 1.0).then_inc(consts_ready, 1)
            pool.memset(ident[:, :], 0.0).then_inc(consts_ready, 1)
            pool.memset(minus_half[:, :], -0.5).then_inc(consts_ready, 1)
            pool.memset(fold[:, :], 0.0).then_inc(consts_ready, 1)
            pool.wait_ge(consts_ready, 4)
            pool.affine_select(out=ident[:, :], in_=ident[:, :], compare_op=ALU.not_equal, fill=1.0,
                               base=0, pattern=[[-1, P]], channel_multiplier=1).then_inc(consts_ready, 1)
            fold_blocks = fold[:, :].rearrange("p (a r) -> p a r", r=SQ)
            for a in range(QUADS):
                pool.affine_select(out=fold_blocks, in_=fold_blocks, compare_op=ALU.not_equal, fill=1.0,
                                   base=-a * SQ, pattern=[[0, QUADS], [-1, SQ]], channel_multiplier=1
                                   ).then_inc(consts_ready, 1)
                pool.wait_ge(consts_ready, 6 + a)
            reciprocal_std(0, 0)
            reciprocal_std(0, 1)
            for c in range(1, CH):
                pool.wait_ge(bk_rows_ready, c + 1)
                if c > 1:
                    pool.wait_ge(wq_bk_ready, c - 1)
                pool.tensor_tensor(wq_bk, bk_rows[0] if c == 1 else wq_bk, bk_rows[c], ALU.add
                                   ).then_inc(wq_bk_ready, 1)
            pool.wait_ge(rstd_ready, 2)
            pool.wait_ge(xn_ready, BPH)
            for n in range(BPH + BY_VECTOR, BLOCKS):
                pool.tensor_scalar(xn[:, n], xn[:, n], mean[:, n:n + 1], rstd[:, n:n + 1],
                                   ALU.subtract, ALU.mult).then_inc(xn_ready, 1)
            for e in range(CH):
                pool.wait_ge(mT_hi_ready, e + 1)
                pool.tensor_tensor(mT_lo[:, e], mT_full[e], mT_hi[:, e].bitcast(F32), ALU.subtract
                                   ).then_inc(mT_lo_ready, 1)
            pool.wait_ge(bv_loaded, 16)
            with pool.Fori(0, B - 1) as b:
                graph(b, True)
            graph(B - 1, False)

        @block.scalar
        def _(act):
            def hidden_hi(b, g):
                act.wait_ge(xnT_ready, GROUPS * b + g + 1)
                half, c = divmod(g, CH)
                act.activation(hT_hi[:, c, half * BANK:(half + 1) * BANK], xnT(b, g), ACT.Relu
                               ).then_inc(hT_hi_ready, 1)

            def graph(b, following):
                for i in range(TILES):
                    act.wait_ge(v_done, TILES * b + i + 1)
                    act.activation(v_hi[:, i], work[:, V_BANK[i]], ACT.Copy).then_inc(v_hi_ready, 1)
                for g in range(GROUPS):
                    act.wait_ge(uT_done, GROUPS * b + g + 1)
                    half, c = divmod(g, CH)
                    act.activation(uT_hi[:, c, half * BANK:(half + 1) * BANK], work[:, U_BANK[g]], ACT.Identity,
                                   bias=a_col[:, c:c + 1]).then_inc(uT_hi_ready, 1)
                act.wait_ge(s_ready, b + 1)
                for u in range(UNITS):
                    i = u % TILES
                    if u >= 2:
                        act.wait_ge(prob_ready, UNITS * b + u - 1)
                    act.wait_ge(scores_done, UNITS * b + u + 1)
                    act.activation(e_sb[:, u % 2], work[:, u % 2], ACT.Exp, bias=s_col[:, i:i + 1]
                                   ).then_inc(exp_ready, 1)
                    act.wait_ge(prob_ready, UNITS * b + u + 1)
                    act.activation(pT_hi[:, u % RING], prob[:, u % RING], ACT.Copy).then_inc(pT_hi_ready, 1)
                    if following and u >= UNITS - CH:
                        hidden_hi(b + 1, u - (UNITS - CH))
                if following:
                    for g in range(CH, GROUPS):
                        hidden_hi(b + 1, g)

            for g in range(2):
                load_first_x(act, 0, g)
            act.dma_start(bq_col[:, :], bq.rearrange("(c p) -> p c", p=P), allow_slow_non_contiguous=True
                          ).then_inc(biases_loaded, 16)
            act.dma_start(bk_col[:, :], bk.rearrange("(c p) -> p c", p=P), allow_slow_non_contiguous=True
                          ).then_inc(biases_loaded, 16)
            for g in range(QUADS):
                load_first_x(act, 1, g)
            act.dma_start(wv_in[:, :, :], wv.rearrange("(c p) d -> p c d", p=P)).then_inc(wv_loaded, 16)
            act.dma_start(bv_rep[:, :], bv.rearrange("(a d) -> a d", a=1).partition_broadcast(P)
                          ).then_inc(bv_loaded, 16)
            act.wait_ge(biases_loaded, 32)
            for e in range(CH):
                if e == CH - 1:
                    for c in range(CH):
                        act.wait_ge(wqk_loaded[c], 32)
                        act.activation(bk_rows[c], wq_in[:, c], ACT.Copy, scale=bk_col[:, c:c + 1]
                                       ).then_inc(bk_rows_ready, 1)
                act.wait_ge(wvT_done, e + 1)
                act.activation(wvT_hi[:, e], work[:, WV_BANK[e]], ACT.Copy).then_inc(wvT_hi_ready, 1)
            for g in range(CH):
                hidden_hi(0, g)
            act.wait_ge(wb_done, 1)
            for g in range(QUADS):
                rows = slice(g * SQ, (g + 1) * SQ)
                act.activation(c_block[rows, :], work[rows, C_BANK, g * P:(g + 1) * P], ACT.Copy)
            act.activation(a_col[:, :], work[:, A_BANK, 0:CH], ACT.Copy)
            act.activation(bqk[:, :], work[:, A_BANK, CH:CH + 1], ACT.Copy).then_inc(wb_ready, 1)
            act.wait_ge(mT_done, 1)
            for e in range(CH):
                act.activation(mT_full[e], o_ps[:, e], ACT.Copy)
                act.activation(mT_hi[:, e], o_ps[:, e], ACT.Copy).then_inc(mT_hi_ready, 1)
            for g in range(CH, GROUPS):
                hidden_hi(0, g)
            act.wait_ge(wb_ready, 1)
            with act.Fori(0, B - 1) as b:
                graph(b, True)
            graph(B - 1, False)

        @block.vector
        def _(dve):
            def row_stats(blocks):
                for n in blocks:
                    dve.bn_stats(stats[:, n], xn[:, n]).then_inc(stats_done, 1)

            def mean_sums(b, half=None):
                blocks = norm_blocks(half)
                dve.wait_ge(stats_done, BLOCKS * b + blocks.stop)
                dve.reduce_sum(block_sum[:, blocks], means[:, blocks], axis=AX.X).then_inc(mean_sum_ready, 1)

            def deviations(b, bank, half=None):
                step = [4 * (norm_no(b, half) - 1)]

                def then_wait(ins):
                    step[0] = step[0] + 1
                    ins.then_inc(var_step_done, 1)
                    dve.wait_ge(var_step_done, step[0])

                parts = 2 * QUADS
                blocks = norm_blocks(half)
                count = blocks.stop - blocks.start
                dve.wait_ge(mean_done, norm_no(b, half))
                then_wait(dve.tensor_scalar(mean[:, blocks], bank[:, MEAN_AT + blocks.start:MEAN_AT + blocks.stop],
                                            1.0 / parts, None, ALU.mult))
                then_wait(dve.tensor_tensor(dev[:, blocks], means[:, blocks],
                                            mean[:, blocks].unsqueeze(2).broadcast_to([P, count, 2]), ALU.subtract))
                then_wait(dve.scalar_tensor_tensor(out=dev_sq[:, blocks], in0=dev[:, blocks], scalar=float(D // parts),
                                                   in1=dev[:, blocks], op0=ALU.mult, op1=ALU.mult))
                then_wait(dve.tensor_tensor(dev_sq[:, blocks], dev_sq[:, blocks], squares[:, blocks], ALU.add))
                dve.reduce_sum(block_sum[:, blocks], dev_sq[:, blocks], axis=AX.X).then_inc(var_sum_ready, 1)

            def variance(b, bank, half=None):
                blocks = norm_blocks(half)
                dve.wait_ge(var_done, norm_no(b, half))
                dve.tensor_scalar(var_eps[:, blocks], bank[:, VAR_AT + blocks.start:VAR_AT + blocks.stop],
                                  1.0 / D, EPS, ALU.mult, ALU.add).then_inc(var_ready, 1)

            def normalise(blocks):
                for n in blocks:
                    dve.tensor_scalar(xn[:, n], xn[:, n], mean[:, n:n + 1], rstd[:, n:n + 1],
                                      ALU.subtract, ALU.mult).then_inc(xn_ready, 1)

            def key_terms(b, blocks):
                for n in blocks:
                    if n == 0:
                        dve.wait_ge(xn_ready, BLOCKS * b + BLOCKS)
                    else:
                        dve.wait_ge(s_block_ready, BLOCKS * b + n)
                    dve.scalar_tensor_tensor(out=spare[:, 0:P], in0=xn[:, n], scalar=0.0, in1=c_block[:, :],
                                             op0=ALU.max, op1=ALU.mult, accum_out=s_block[:, n:n + 1]
                                             ).then_inc(s_block_ready, 1)

            def key_bias(b):
                dve.wait_ge(s_done, b + 1)
                sums = o_ps[:, 0, 0:BLOCKS].rearrange("p (i a) -> p i a", a=QUADS)
                for a in range(QUADS):
                    rows = slice(a * SQ, (a + 1) * SQ)
                    last = dve.tensor_scalar(s_col[rows, :], sums[rows, :, a], bqk[rows, 0:1], None, ALU.add)
                last.then_inc(s_ready, 1)

            def transpose_xn(b, g):
                half, c = divmod(g, CH)
                dve.wait_ge(xn_ready, BLOCKS * b + BPH * (half + 1))
                first = isinstance(b, int) and b == 0
                if first and g == 2:
                    dve.wait_ge(wq_bk_ready, CH - 1)
                if (g >= 1 and not first) or g >= RING:
                    dve.wait_ge(hT_lo_ready, GROUPS * b + (g if g < CH else g - RING + 1))
                if g >= CH and not first:
                    dve.wait_ge(sum_ready, summed(b - 1, UNITS - RING + g % RING))
                    dve.wait_ge(pT_lo_ready, UNITS * b - RING + g % RING + 1)
                blocks = xn[:, half * BPH:(half + 1) * BPH].rearrange("p n (r e) -> p n r e", e=CH)
                dve.transpose(xnT(b, g).rearrange("p (n c) -> p n c", c=SQ), blocks[:, :, :, c]
                              ).then_inc(xnT_ready, 1)

            def hidden_lo(b, g):
                dve.wait_ge(hT_hi_ready, GROUPS * b + g + 1)
                half, c = divmod(g, CH)
                cols = slice(half * BANK, (half + 1) * BANK)
                dve.scalar_tensor_tensor(out=hT_lo[:, c, cols], in0=xnT(b, g), scalar=0.0,
                                         in1=hT_hi[:, c, cols].bitcast(F32), op0=ALU.max, op1=ALU.subtract
                                         ).then_inc(hT_lo_ready, 1)

            def hidden_half(b, half):
                groups = range(half * CH, (half + 1) * CH)
                transpose_xn(b, groups[0])
                for g in groups:
                    if g + 1 in groups:
                        transpose_xn(b, g + 1)
                    hidden_lo(b, g)

            def transpose_adj(b, u):
                queries, i = divmod(u, TILES)
                keys, m = divmod(i, TPH)
                if m == 0:
                    dve.wait_ge(adj_loaded[keys], 16 * QUADS * (HALVES * b + queries + 1))
                if u >= RING:
                    dve.wait_ge(sum_ready, summed(b, u - RING))
                    dve.wait_ge(pT_lo_ready, UNITS * b + u - RING + 1)
                dve.transpose(prob[:, u % RING].rearrange("p (n c) -> p n c", c=SQ),
                              adj_in[:, keys].rearrange("p n (r m) -> p n r m", m=TPH)[:, :, :, m]
                              ).then_inc(adjT_ready, 1)

            def quadrant_sums(b, half):
                dve.wait_ge(sum_ready, summed(b, TILES * (half + 1) - 1))
                dve.transpose(spare[:, :].rearrange("p (n c) -> p n c", c=SQ),
                              prob_sum[:, :].rearrange("p (n r) -> p n r", r=SQ)).then_inc(sumT_done, 1)
                dve.wait_ge(sumT_done, HALVES * b + half + 1)
                dve.reduce_sum(quad_sum[:, :], spare[:, :].rearrange("p (n c) -> p n c", c=SQ), axis=AX.X
                               ).then_inc(quad_sum_ready, 1)

            def results(b, half):
                dve.wait_ge(row_sums_done, HALVES * b + half + 1)
                sums = work[:, SUM_BANK, half * TPH * QUADS:(half + 1) * TPH * QUADS].rearrange(
                    "p (m a) -> p m a", a=QUADS)
                for a in range(QUADS):
                    rows = slice(a * SQ, (a + 1) * SQ)
                    last = dve.reciprocal(row_inv[rows, half * TPH:(half + 1) * TPH], sums[rows, :, a])
                last.then_inc(row_inv_ready, 1)
                dve.wait_ge(row_inv_ready, HALVES * b + half + 1)
                for m in range(TPH):
                    n = half * TPH + m
                    dve.wait_ge(res_bv_ready, TILES * b + n + 1)
                    dve.wait_ge(o_done, TILES * b + n + 1)
                    dve.scalar_tensor_tensor(out=res[:, m], in0=o_ps[:, m], scalar=row_inv[:, n:n + 1],
                                             in1=res[:, m], op0=ALU.mult, op1=ALU.add).then_inc(out_ready, 1)

            def graph(b, following):
                for i in range(TILES):
                    dve.wait_ge(v_hi_ready, TILES * b + i + 1)
                    dve.tensor_tensor(v_lo[:, i], work[:, V_BANK[i]], v_hi[:, i].bitcast(F32),
                                      ALU.subtract).then_inc(v_lo_ready, 1)
                    key_terms(b, range(i * QUADS, (i + 1) * QUADS))
                for g in range(GROUPS):
                    dve.wait_ge(uT_hi_ready, GROUPS * b + g + 1)
                    half, c = divmod(g, CH)
                    cols = slice(half * BANK, (half + 1) * BANK)
                    dve.scalar_tensor_tensor(out=uT_lo[:, c, cols], in0=work[:, U_BANK[g]],
                                             scalar=a_col[:, c:c + 1], in1=uT_hi[:, c, cols].bitcast(F32),
                                             op0=ALU.add, op1=ALU.subtract).then_inc(uT_lo_ready, 1)
                    if g < 2:
                        transpose_adj(b, g)
                    if g == CH:
                        key_bias(b)
                for u in range(UNITS):
                    dve.wait_ge(exp_ready, UNITS * b + u + 1)
                    dve.wait_ge(adjT_ready, UNITS * b + u + 1)
                    dve.tensor_tensor(prob[:, u % RING], e_sb[:, u % 2], prob[:, u % RING], ALU.mult
                                      ).then_inc(prob_ready, 1)
                    if u + 2 < UNITS:
                        transpose_adj(b, u + 2)
                    if following and u >= UNITS - CH:
                        transpose_xn(b + 1, u - (UNITS - CH))
                    if following and u == NORMALISED[0]:
                        dve.wait_ge(rstd_ready, norm_no(b + 1))
                    dve.wait_ge(pT_hi_ready, UNITS * b + u + 1)
                    dve.tensor_tensor(pT_lo[:, u % RING], prob[:, u % RING], pT_hi[:, u % RING].bitcast(F32),
                                      ALU.subtract).then_inc(pT_lo_ready, 1)
                    if following:
                        if u in (0, 2):
                            dve.wait_ge(x_loaded[u // 2], 16 * QUADS * b + 2 * 16 * QUADS)
                        if u < 4:
                            row_stats(range(u * TILES, (u + 1) * TILES))
                        if u == 4:
                            mean_sums(b + 1)
                        if u == 6:
                            deviations(b + 1, work[:, SUM_BANK])
                        if u == 7:
                            variance(b + 1, work[:, SUM_BANK])
                        if u in NORMALISED:
                            n = NORMALISED.index(u) * TILES
                            normalise(range(n, n + TILES))
                        if u >= UNITS - CH:
                            hidden_lo(b + 1, u - (UNITS - CH))
                    if u == TILES:
                        quadrant_sums(b, 0)
                    if u == TILES + LAG - 1:
                        results(b, 0)
                if following:
                    dve.wait_ge(hT_lo_ready, GROUPS * (b + 1) + CH)
                quadrant_sums(b, 1)
                if following:
                    hidden_half(b + 1, 1)
                results(b, 1)

            def wvT_low(e):
                dve.wait_ge(wvT_hi_ready, e + 1)
                dve.tensor_tensor(wvT_lo[:, e], work[:, WV_BANK[e]], wvT_hi[:, e].bitcast(F32), ALU.subtract
                                  ).then_inc(wvT_lo_ready, 1)

            sum_bank = work[:, SUM_BANK_0]
            dve.wait_ge(x_loaded[0], 16 * QUADS)
            row_stats(range(BPH))
            mean_sums(0, 0)
            deviations(0, sum_bank, 0)
            dve.wait_ge(consts_ready, 1)
            dve.wait_ge(biases_loaded, 32)
            for c in range(CH):
                last = dve.tensor_scalar(bq_rep[:, c], ones[:, :], bq_col[:, c:c + 1], None, ALU.mult)
            last.then_inc(bq_rep_ready, 1)
            variance(0, sum_bank, 0)
            dve.wait_ge(x_loaded[1], 16 * QUADS)
            row_stats(range(BPH, BLOCKS))
            mean_sums(0, 1)
            deviations(0, sum_bank, 1)
            variance(0, sum_bank, 1)
            dve.wait_ge(rstd_ready, 1)
            normalise(range(QUADS))
            for e in range(3):
                wvT_low(e)
            normalise(range(QUADS, BPH))
            wvT_low(3)
            hidden_half(0, 0)
            dve.wait_ge(rstd_ready, 2)
            normalise(range(BPH, BPH + BY_VECTOR))
            hidden_half(0, 1)
            dve.wait_ge(mT_lo_ready, CH)
            dve.wait_ge(wb_ready, 1)
            with dve.Fori(0, B - 1) as b:
                graph(b, True)
            graph(B - 1, False)

        @block.tensor
        def _(pe):
            def product(out_ps, lhs_hi, lhs_lo, rhs_hi, rhs_lo, first, last):
                pe.matmul(out_ps, lhs_hi, rhs_hi, start=first, stop=False)
                pe.matmul(out_ps, lhs_hi, rhs_lo, start=False, stop=False)
                return pe.matmul(out_ps, lhs_lo, rhs_hi, start=False, stop=last)

            def fold_blocks(bank, at, half):
                blocks = norm_blocks(half)
                return pe.matmul(bank[:, at + blocks.start:at + blocks.stop], fold[:, :], block_sum[:, blocks],
                                 start=True, stop=True)

            def fold_means(b, bank, half=None):
                pe.wait_ge(mean_sum_ready, norm_no(b, half))
                fold_blocks(bank, MEAN_AT, half).then_inc(mean_done, 1)

            def fold_variances(b, bank, half=None):
                pe.wait_ge(var_sum_ready, norm_no(b, half))
                fold_blocks(bank, VAR_AT, half).then_inc(var_done, 1)

            def scores(b, u):
                if u < 2:
                    pe.wait_ge(uT_lo_ready, GROUPS * b + U_BANK.index(u, 4) + 1)
                else:
                    pe.wait_ge(exp_ready, UNITS * b + u - 1)
                half, i = divmod(u, TILES)
                if u == TPH:
                    pe.wait_ge(uT_lo_ready, GROUPS * b + GROUPS)
                keys = slice(i * P, (i + 1) * P)
                queries = slice(half * BANK, (half + 1) * BANK)
                for c in range(CH):
                    last = product(work[:, u % 2], uT_hi[:, c, keys], uT_lo[:, c, keys],
                                   hT_hi[:, c, queries], hT_lo[:, c, queries], c == 0, c == CH - 1)
                last.then_inc(scores_done, 1)

            def row_sums(b, half):
                pe.wait_ge(quad_sum_ready, HALVES * b + half + 1)
                at = half * TPH * QUADS
                pe.matmul(work[:, SUM_BANK, at:at + TPH * QUADS], fold[:, :], quad_sum[:, :],
                          start=True, stop=True).then_inc(row_sums_done, 1)

            def weighted_sum(b, u):
                half, i = divmod(u, TILES)
                pe.wait_ge(pT_lo_ready, UNITS * b + u + 1)
                for m in range(TPH):
                    if half and i == 0:
                        pe.wait_ge(out_ready, TILES * b + m + 1)
                    last = product(o_ps[:, m], pT_hi[:, u % RING, m * P:(m + 1) * P],
                                   pT_lo[:, u % RING, m * P:(m + 1) * P],
                                   v_hi[:, i], v_lo[:, i], i == 0, i == TILES - 1)
                    if i == TILES - 1:
                        last.then_inc(o_done, 1)

            def graph(b, following):
                for i in range(TILES):
                    if i % TPH == 0:
                        pe.wait_ge(hT_lo_ready, GROUPS * b + CH * (i // TPH + 1))
                    if i == 3:
                        pe.wait_ge(v_lo_ready, TILES * b + 1)
                    elif i >= 4:
                        pe.wait_ge(v_lo_ready, TILES * b + i - 3)
                    rows = slice(i * P, (i + 1) * P)
                    for c in range(CH):
                        last = product(work[:, V_BANK[i]], hT_hi[:, c, rows], hT_lo[:, c, rows],
                                       wvT_hi[:, c], wvT_lo[:, c], c == 0, c == CH - 1)
                    last.then_inc(v_done, 1)
                pe.wait_ge(mT_lo_ready, CH)
                for g in range(GROUPS):
                    half, c_out = divmod(g, CH)
                    if g < 4:
                        pe.wait_ge(v_lo_ready, TILES * b + TILES - 3 + g)
                    else:
                        pe.wait_ge(uT_lo_ready, GROUPS * b + g - 3)
                    cols = slice(half * BANK, (half + 1) * BANK)
                    outs = slice(c_out * P, (c_out + 1) * P)
                    for c in range(CH):
                        last = product(work[:, U_BANK[g]], mT_hi[:, c, outs], mT_lo[:, c, outs],
                                       hT_hi[:, c, cols], hT_lo[:, c, cols], c == 0, c == CH - 1)
                    last.then_inc(uT_done, 1)
                    if g == 2:
                        pe.wait_ge(s_block_ready, BLOCKS * b + BLOCKS)
                        pe.matmul(o_ps[:, 0, 0:BLOCKS], fold[:, :], s_block[:, :], start=True, stop=True
                                  ).then_inc(s_done, 1)
                for u in range(UNITS):
                    scores(b, u)
                    if following and u == 5:
                        fold_means(b + 1, work[:, SUM_BANK])
                    if following and u == 7:
                        fold_variances(b + 1, work[:, SUM_BANK])
                    if u == TILES + 2:
                        row_sums(b, 0)
                    if u >= LAG:
                        weighted_sum(b, u - LAG)
                weighted_sum(b, UNITS - 3)
                weighted_sum(b, UNITS - 2)
                row_sums(b, 1)
                weighted_sum(b, UNITS - 1)

            def by_feature(w, c):
                return w[:, c].rearrange("o (p e) -> o e p", e=CH)

            def weight_product(c, outs=range(CH)):
                pe.wait_ge(wqk_loaded[c], 32)
                for e in outs:
                    last = pe.matmul(o_ps[:, e], by_feature(wk_in, c)[:, e], by_feature(wq_in, c),
                                     start=(c == 0), stop=(c == CH - 1))
                if c == CH - 1 and outs.stop == CH:
                    last.then_inc(mT_done, 1)

            def transpose_wv(e):
                for c in range(CH):
                    last = pe.transpose(work[:, WV_BANK[e], c * P:(c + 1) * P], by_feature(wv_in, c)[:, e],
                                        ident[:, :])
                last.then_inc(wvT_done, 1)

            sum_bank = work[:, SUM_BANK_0]
            weight_product(0)
            pe.wait_ge(consts_ready, 9)
            fold_means(0, sum_bank, 0)
            weight_product(1, range(2))
            fold_variances(0, sum_bank, 0)
            weight_product(1, range(2, CH))
            weight_product(2, range(2))
            pe.wait_ge(var_ready, 1)
            fold_means(0, sum_bank, 1)
            pe.wait_ge(wv_loaded, 16)
            for e in range(3):
                transpose_wv(e)
            fold_variances(0, sum_bank, 1)
            weight_product(2, range(2, CH))
            pe.wait_ge(wvT_lo_ready, 1)
            transpose_wv(3)
            pe.wait_ge(bq_rep_ready, 1)
            pe.wait_ge(wqk_loaded[CH - 1], 32)
            pe.wait_ge(wvT_lo_ready, 2)
            for c in range(CH):
                pe.matmul(work[:, C_BANK], bq_rep[:, c], wk_in[:, c], start=(c == 0), stop=(c == CH - 1))
            weight_product(3, range(3))
            pe.wait_ge(wvT_lo_ready, 3)
            pe.wait_ge(wq_bk_ready, CH - 1)
            for e in range(CH):
                pe.matmul(work[:, A_BANK, e:e + 1], wq_bk.rearrange("o (p e) -> o e p", e=CH)[:, e], ones[:, 0:1],
                          start=True, stop=True)
            for c in range(CH):
                last = pe.matmul(work[:, A_BANK, CH:CH + 1], bq_rep[:, c], bk_col[:, c:c + 1],
                                 start=(c == 0), stop=(c == CH - 1))
            last.then_inc(wb_done, 1)
            weight_product(3, range(3, CH))
            pe.wait_ge(wvT_lo_ready, CH)
            pe.wait_ge(wb_ready, 1)
            pe.wait_ge(var_ready, HALVES)
            with pe.Fori(0, B - 1) as b:
                graph(b, True)
            graph(B - 1, False)


_INS = ['x', 'adj', 'L0_gnn_Wq_w', 'L0_gnn_Wq_b', 'L0_gnn_Wk_w', 'L0_gnn_Wk_b', 'L0_gnn_Wv_w', 'L0_gnn_Wv_b']


def kernel(**inputs):
    import numpy as _np
    import concourse.bacc as _bacc
    from concourse import mybir as _mybir
    from concourse.bass_utils import run_bass_kernel_spmd as _run

    nc = _bacc.Bacc("TRN2", target_bir_lowering=False, num_devices=1)
    arrays, args = {}, []
    for name in _INS:
        a = _np.ascontiguousarray(inputs[name])
        arrays[f"in_{name}_dram"] = a
        args.append(nc.dram_tensor(f"in_{name}_dram", a.shape, _mybir.dt.from_np(a.dtype), kind="ExternalInput").ap())
    shape = tuple(inputs['x'].shape)
    args.append(nc.dram_tensor("out_0_dram", shape, _mybir.dt.float32, kind="ExternalOutput").ap())
    adjacency_attention_kernel(nc, *args)
    r = _run(nc, [arrays], core_ids=[0])
    return r.results[0]["out_0_dram"]
```
